# Optimizing a Trainium2 kernel written in Bass

```python
import numpy as np
import jax
import jax.numpy as jnp

def _softmax(x, axis=-1):
    return jax.nn.softmax(x, axis=axis)

def _gelu(x):
    return jax.nn.gelu(x, approximate=True)

def _silu(x):
    return jax.nn.silu(x)

def _sigmoid(x):
    return jax.nn.sigmoid(x)

def _layernorm(x, axis=-1, eps=1e-05):
    m = jnp.mean(x, axis=axis, keepdims=True)
    v = jnp.var(x, axis=axis, keepdims=True)
    return (x - m) / jnp.sqrt(v + eps)

def _scatter_add(tgt, idx, src, axis=0):
    return tgt.at[idx].add(src)

def _segment_sum(src, seg, n):
    return jax.ops.segment_sum(src, seg, n)
kernel_name = 'mk_seq_preln_d1_jaxref_r8_c9708e'

def setup_inputs(seed: int=0):
    np.random.seed(seed)
    _w = jnp.asarray

    def _L0_attn_setup():
        import jax, jax.numpy as jnp
        import numpy as np
        B, L, D, FF = (4, 512, 128, 512)
        EPS = 1e-05

        def _layernorm(x, gamma, beta):
            mu = jnp.mean(x, axis=-1, keepdims=True)
            var = jnp.var(x, axis=-1, keepdims=True)
            return (x - mu) * jax.lax.rsqrt(var + EPS) * gamma + beta

        def _spiral_conv(x, phazor_re, phazor_im, phazor_init_re, phazor_init_im, last_conv_re, last_conv_im):
            length = x.shape[1]
            phazor_raw = phazor_re + 1j * phazor_im
            mag = jnp.abs(phazor_raw)
            phazor = phazor_raw / mag * jnp.exp(-mag)
            t = jnp.arange(length)[:, None]
            prog = jnp.power(phazor[None, :], t)
            phazor_init = phazor_init_re + 1j * phazor_init_im
            filt = prog * phazor_init[None, :]
            filt_fft = jnp.fft.fft(filt, n=2 * length, axis=0)
            x_fft = jnp.fft.fft(x.astype(jnp.complex64), n=2 * length, axis=1)
            conv = jnp.fft.ifft(filt_fft[None] * x_fft, axis=1)[:, :length]
            last_conv = last_conv_re + 1j * last_conv_im
            last_conv = jax.lax.stop_gradient(last_conv)
            conv_with_past = conv + last_conv[None, None, :] * prog[None] * phazor[None, None, :]
            return conv_with_past.real
        key = jax.random.key(seed)
        ks = jax.random.split(key, 10)
        return {'x': jax.random.normal(ks[0], (B, L, D), dtype=jnp.float32), 'ln_gamma': jnp.ones((D,), dtype=jnp.float32), 'ln_beta': jnp.zeros((D,), dtype=jnp.float32), 'phazor_re': jax.random.normal(ks[1], (D,), dtype=jnp.float32), 'phazor_im': jax.random.normal(ks[2], (D,), dtype=jnp.float32), 'phazor_init_re': jax.random.normal(ks[3], (D,), dtype=jnp.float32), 'phazor_init_im': jax.random.normal(ks[4], (D,), dtype=jnp.float32), 'last_conv_re': jax.random.normal(ks[5], (D,), dtype=jnp.float32), 'last_conv_im': jax.random.normal(ks[6], (D,), dtype=jnp.float32), 'w1': jax.random.normal(ks[7], (D, FF), dtype=jnp.float32) * 0.02, 'b1': jnp.zeros((FF,), dtype=jnp.float32), 'w2': jax.random.normal(ks[8], (FF, D), dtype=jnp.float32) * 0.02, 'b2': jnp.zeros((D,), dtype=jnp.float32)}
    _L0_attn_in = _L0_attn_setup()

    def _L0_ffn_setup():
        import jax, jax.numpy as jnp
        import numpy as np
        S, B, H, F, E, K = (256, 2, 128, 256, 8, 2)

        def _moe_forward(hidden_states, router_w, w1, b1, w2, b2):
            s, b, h = hidden_states.shape
            T = s * b
            x = hidden_states.reshape(T, h)
            logits = jnp.einsum('th,eh->te', x, router_w)
            topk_logits, topk_idx = jax.lax.top_k(logits, K)
            probs = jax.nn.softmax(topk_logits, axis=-1)
            combine = jnp.zeros((T, E), dtype=x.dtype)
            combine = combine.at[jnp.arange(T)[:, None], topk_idx].add(probs.astype(x.dtype))
            hmid = jnp.einsum('th,efh->etf', x, w1) + b1[:, None, :]
            hmid = jax.nn.gelu(hmid, approximate=False)
            y = jnp.einsum('etf,ehf->eth', hmid, w2) + b2[:, None, :]
            out = jnp.einsum('eth,te->th', y, combine)
            return out.reshape(s, b, h)
        key = jax.random.key(seed)
        ks = jax.random.split(key, 6)
        std = 0.02
        return {'hidden_states': jax.random.normal(ks[0], (S, B, H), dtype=jnp.float32), 'router_w': jax.random.normal(ks[1], (E, H), dtype=jnp.float32) * std, 'w1': jax.random.normal(ks[2], (E, F, H), dtype=jnp.float32) * (1.0 / np.sqrt(H)), 'b1': jnp.zeros((E, F), dtype=jnp.float32), 'w2': jax.random.normal(ks[3], (E, H, F), dtype=jnp.float32) * (1.0 / np.sqrt(F)), 'b2': jnp.zeros((E, H), dtype=jnp.float32)}
    _L0_ffn_in = _L0_ffn_setup()
    _d = {'L0_attn_x': _L0_attn_in['x'], 'L0_attn_ln_gamma': _L0_attn_in['ln_gamma'], 'L0_attn_ln_beta': _L0_attn_in['ln_beta'], 'L0_attn_phazor_re': _L0_attn_in['phazor_re'], 'L0_attn_phazor_im': _L0_attn_in['phazor_im'], 'L0_attn_phazor_init_re': _L0_attn_in['phazor_init_re'], 'L0_attn_phazor_init_im': _L0_attn_in['phazor_init_im'], 'L0_attn_last_conv_re': _L0_attn_in['last_conv_re'], 'L0_attn_last_conv_im': _L0_attn_in['last_conv_im'], 'L0_attn_w1': _L0_attn_in['w1'], 'L0_attn_b1': _L0_attn_in['b1'], 'L0_attn_w2': _L0_attn_in['w2'], 'L0_attn_b2': _L0_attn_in['b2'], 'L0_ffn_router_w': _L0_ffn_in['router_w'], 'L0_ffn_w1': _L0_ffn_in['w1'], 'L0_ffn_b1': _L0_ffn_in['b1'], 'L0_ffn_w2': _L0_ffn_in['w2'], 'L0_ffn_b2': _L0_ffn_in['b2']}
    _x0 = _d['L0_attn_x']
    _d['L0_attn_x'] = jax.random.normal(jax.random.fold_in(jax.random.key(seed), 1), (8, 1024, 128), dtype=_x0.dtype)
    del _x0
    return _d

def reference(L0_attn_x, L0_attn_ln_gamma, L0_attn_ln_beta, L0_attn_phazor_re, L0_attn_phazor_im, L0_attn_phazor_init_re, L0_attn_phazor_init_im, L0_attn_last_conv_re, L0_attn_last_conv_im, L0_attn_w1, L0_attn_b1, L0_attn_w2, L0_attn_b2, L0_ffn_router_w, L0_ffn_w1, L0_ffn_b1, L0_ffn_w2, L0_ffn_b2):

    def _L0_attn_ref(x, ln_gamma, ln_beta, phazor_re, phazor_im, phazor_init_re, phazor_init_im, last_conv_re, last_conv_im, w1, b1, w2, b2):
        import jax, jax.numpy as jnp
        import numpy as np
        B, L, D, FF = (4, 512, 128, 512)
        EPS = 1e-05

        def _layernorm(x, gamma, beta):
            mu = jnp.mean(x, axis=-1, keepdims=True)
            var = jnp.var(x, axis=-1, keepdims=True)
            return (x - mu) * jax.lax.rsqrt(var + EPS) * gamma + beta

        def _spiral_conv(x, phazor_re, phazor_im, phazor_init_re, phazor_init_im, last_conv_re, last_conv_im):
            length = x.shape[1]
            phazor_raw = phazor_re + 1j * phazor_im
            mag = jnp.abs(phazor_raw)
            phazor = phazor_raw / mag * jnp.exp(-mag)
            t = jnp.arange(length)[:, None]
            prog = jnp.power(phazor[None, :], t)
            phazor_init = phazor_init_re + 1j * phazor_init_im
            filt = prog * phazor_init[None, :]
            filt_fft = jnp.fft.fft(filt, n=2 * length, axis=0)
            x_fft = jnp.fft.fft(x.astype(jnp.complex64), n=2 * length, axis=1)
            conv = jnp.fft.ifft(filt_fft[None] * x_fft, axis=1)[:, :length]
            last_conv = last_conv_re + 1j * last_conv_im
            last_conv = jax.lax.stop_gradient(last_conv)
            conv_with_past = conv + last_conv[None, None, :] * prog[None] * phazor[None, None, :]
            return conv_with_past.real
        h = _layernorm(x, ln_gamma, ln_beta)
        h = _spiral_conv(h, phazor_re, phazor_im, phazor_init_re, phazor_init_im, last_conv_re, last_conv_im)
        x1 = h + x
        h = _layernorm(x1, ln_gamma, ln_beta)
        h = jax.nn.silu(h @ w1 + b1) @ w2 + b2
        return h + x1

    def _L0_ffn_ref(hidden_states, router_w, w1, b1, w2, b2):
        import jax, jax.numpy as jnp
        import numpy as np
        S, B, H, F, E, K = (256, 2, 128, 256, 8, 2)

        def _moe_forward(hidden_states, router_w, w1, b1, w2, b2):
            s, b, h = hidden_states.shape
            T = s * b
            x = hidden_states.reshape(T, h)
            logits = jnp.einsum('th,eh->te', x, router_w)
            topk_logits, topk_idx = jax.lax.top_k(logits, K)
            probs = jax.nn.softmax(topk_logits, axis=-1)
            combine = jnp.zeros((T, E), dtype=x.dtype)
            combine = combine.at[jnp.arange(T)[:, None], topk_idx].add(probs.astype(x.dtype))
            hmid = jnp.einsum('th,efh->etf', x, w1) + b1[:, None, :]
            hmid = jax.nn.gelu(hmid, approximate=False)
            y = jnp.einsum('etf,ehf->eth', hmid, w2) + b2[:, None, :]
            out = jnp.einsum('eth,te->th', y, combine)
            return out.reshape(s, b, h)
        return _moe_forward(hidden_states, router_w, w1, b1, w2, b2)
    x = L0_attn_x
    x = x + _L0_attn_ref(_layernorm(x, axis=-1), L0_attn_ln_gamma, L0_attn_ln_beta, L0_attn_phazor_re, L0_attn_phazor_im, L0_attn_phazor_init_re, L0_attn_phazor_init_im, L0_attn_last_conv_re, L0_attn_last_conv_im, L0_attn_w1, L0_attn_b1, L0_attn_w2, L0_attn_b2)
    x = x + _L0_ffn_ref(_layernorm(x, axis=-1), L0_ffn_router_w, L0_ffn_w1, L0_ffn_b1, L0_ffn_w2, L0_ffn_b2)
    return x

_drawn_inputs = setup_inputs


def setup_inputs(seed=0):
    import zlib

    import numpy as np

    out = dict(_drawn_inputs(seed))
    spreads = {'L0_attn_ln_gamma': (1.0, 0.2),
     'L0_attn_ln_beta': (0.0, 0.1),
     'L0_attn_b1': (0.0, 0.334),
     'L0_attn_b2': (0.0, 0.1),
     'L0_ffn_b1': (0.0, 0.386),
     'L0_ffn_b2': (0.0, 0.269)}
    factors = {'L0_attn_last_conv_re': 5.383, 'L0_attn_last_conv_im': 8.0}
    for name, (base, spread) in spreads.items():
        noise = np.random.default_rng([zlib.crc32(name.encode()), seed]).standard_normal(out[name].shape)
        drawn = base * np.exp(spread * noise) if base else spread * noise
        out[name] = jnp.asarray(drawn.astype(out[name].dtype))
    for name, factor in factors.items():
        out[name] = (out[name] * factor).astype(out[name].dtype)
    return out
```

```python
import concourse.bass as bass
from concourse import mybir
from contextlib import ExitStack

BATCHES, LENGTH, D = 8, 1024, 128
FF = 512
EXPERTS, EF = 8, 256
TILE = 128
TPB = LENGTH // TILE
TILES = BATCHES * TPB
HALF = 512
FC = FF // 128
EC = EF // 128
EPS = 1e-5
(GAMMA, BETA, P_RE, P_IM, INIT_RE, INIT_IM, LAST_RE, LAST_IM) = range(8)
B1 = 8
MB1 = B1 + FC
COLS = MB1 + EXPERTS * EC
EXP_HALVINGS = 7
EXP_DEGREE = 10
EXP_LARGEST = 104.0
LARGE = 3.0e38


def block_moe_kernel(nc, x, cols, w1, w2, b2, router, mw1, mw2, mb2, out):
    f32 = mybir.dt.float32
    f32r = mybir.dt.float32r
    ALU = mybir.AluOpType
    ACT = mybir.ActivationFunctionType
    AX = mybir.AxisListType.X

    x_dram = x.rearrange("b (j p) d -> b p j d", p=TILE)
    out_dram = out.rearrange("b (j p) d -> b p j d", p=TILE)

    ctx = ExitStack()
    with ctx:
        def sb(name, shape, dt=f32):
            return ctx.enter_context(nc.sbuf_tensor(name, shape, dt))

        def sem(name):
            return ctx.enter_context(nc.semaphore(name))

        resid = sb("resid", [128, TILES, D])
        xm_hi = sb("xm_hi", [128, BATCHES * LENGTH], f32r)
        xm_lo = sb("xm_lo", [128, BATCHES * LENGTH], f32r)
        par = sb("par", [128, COLS])
        w1_sb = sb("w1_sb", [128, FF])
        w1_hi = sb("w1_hi", [128, FF], f32r)
        w1_lo = sb("w1_lo", [128, FF], f32r)
        w2_sb = sb("w2_sb", [128, FC, D])
        b2_all = sb("b2_all", [128, 1, D])
        mw1_sb = sb("mw1_sb", [128, EXPERTS * EF])
        mw1_hi = sb("mw1_hi", [128, EXPERTS * EF], f32r)
        mw1_lo = sb("mw1_lo", [128, EXPERTS * EF], f32r)
        mw2_sb = sb("mw2_sb", [128, EXPERTS * EC, D])
        mb2_sb = sb("mb2_sb", [EXPERTS, D])
        router_sb = sb("router_sb", [128, EXPERTS])
        router_hi = sb("router_hi", [128, 128], f32r)
        router_lo = sb("router_lo", [128, 128], f32r)
        ident = sb("ident", [128, 128])
        rank = sb("rank", [128, 1, EXPERTS])
        in_re = sb("in_re", [128, LENGTH])
        in_im = sb("in_im", [128, LENGTH])
        out_re = sb("out_re", [128, LENGTH])
        out_im = sb("out_im", [128, LENGTH])
        cst = sb("cst", [128, 64])
        yk = sb("yk", [128, EXP_DEGREE])
        hn = sb("hn", [128, TPB, D])
        u = sb("u", [128, LENGTH])
        vr = sb("vr", [128, LENGTH])
        vi = sb("vi", [128, LENGTH])
        x1 = sb("x1", [128, TPB, D])
        h2 = sb("h2", [128, TPB, D])
        h_hi = sb("h_hi", [128, LENGTH], f32r)
        h_lo = sb("h_lo", [128, LENGTH], f32r)
        act = [[sb(f"act{a}{c}", [128, LENGTH]) for c in range(2)] for a in range(2)]
        stats = sb("stats", [128, TPB, 6])
        mom0 = sb("mom0", [128, TPB, 2])
        mom1 = sb("mom1", [128, TPB, 2])
        mom2 = sb("mom2", [128, TPB, 2])
        half_pow = sb("half_pow", [128, TPB])
        neg_half = sb("neg_half", [128, TPB])
        eps = sb("eps", [128, TPB])
        neg_one = sb("neg_one", [128, TPB])
        tmp = sb("tmp", [128, 4, TPB])
        scale0 = sb("scale0", [128, TPB])
        unscale0 = sb("unscale0", [128, TPB])
        scale1 = sb("scale1", [128, TPB])
        shift1 = sb("shift1", [128, TPB])
        negmean1 = sb("negmean1", [128, TPB])
        scale2 = sb("scale2", [128, TPB])
        logit_t = [hn[0:EXPERTS, :, :].rearrange("p a b -> p (a b)"), u[0:EXPERTS, :]]
        comb_t = [vr[0:EXPERTS, :], vi[0:EXPERTS, :]]
        TE = TILES * EXPERTS

        def te(t, k):
            return t[:, k * TE:(k + 1) * TE].rearrange("p (t e) -> p t e", e=EXPERTS)
        x1_flat = x1[:, :, :].rearrange("p a b -> p (a b)")
        h2_flat = h2[:, :, :].rearrange("p a b -> p (a b)")
        logits = te(x1_flat, 0)
        first = te(x1_flat, 1)
        second = te(h2_flat, 0)
        scored = te(h2_flat, 1)
        comb_buf = sb("comb", [128, TILES, EXPERTS])
        comb = comb_buf[:, :, :]
        best = sb("best", [128, TILES, 1])
        runner = sb("runner", [128, TILES, 1])
        pick = sb("pick", [128, TILES, 1])
        th = sb("th", [128, TILES, 1])
        prob1 = sb("prob1", [128, TILES, 1])
        prob2 = sb("prob2", [128, TILES, 1])
        acc = x1
        comb_n = sb("comb_n", [128, TPB, EXPERTS])
        spare_v = sb("spare_v", [128, 1])
        spare_p = sb("spare_p", [128, 1])
        b1_all = sb("b1_all", [128, FC])
        act_xm = act[1][0][:, :].rearrange("p (j d) -> p j d", d=D)

        def pair(name):
            return ctx.enter_context(nc.psum_tensor(name, [128, LENGTH], f32))
        trans_p = pair("trans_p")
        up_p = [pair("up_p0"), pair("up_p1")]
        down_p = pair("down_p")
        moe_p = [down_p, trans_p]

        s_par = sem("params_loaded")
        s_w = sem("weights_loaded")
        s_mw = sem("expert_weights_loaded")
        s_x = sem("x_loaded")
        s_store = sem("block_stored")
        s_ident = sem("identity_ready")
        s_pow = sem("powers_ready")
        s_pc = sem("pool_const_order")
        s_po = sem("pool_order")
        s_vc = sem("vector_const_order")
        s_tab = sem("tables_ready")
        s_wsplit = sem("weights_split")
        s_b1raw = sem("bias_product_done")
        s_b1 = sem("bias_ready")
        s_vo = sem("vector_order")
        s_mag = sem("magnitude_ready")
        s_x0m = sem("x0_moments")
        s_sc0 = sem("x0_scales")
        s_hn = sem("hn_ready")
        s_t1 = sem("hn_transposed")
        s_u = sem("u_ready")
        s_ur = sem("u_re_ready")
        s_ui = sem("u_im_ready")
        s_vi = sem("v_im_ready")
        s_ti = sem("out_im_ready")
        s_conv = sem("conv_ready")
        s_t2 = sem("conv_transposed")
        s_x1 = sem("x1_ready")
        s_x1m = sem("x1_moments")
        s_sc1 = sem("x1_scales")
        s_h2 = sem("h2_ready")
        s_base = sem("residual_ready")
        s_t3 = sem("h2_transposed")
        s_hi = sem("h_hi_ready")
        s_lo = sem("h_lo_ready")
        s_up = sem("up_done")
        s_silu = sem("silu_done")
        s_dn = sem("down_done")
        s_x2 = sem("x2_ready")
        s_x2m = sem("x2_moments")
        s_sc2 = sem("x2_scales")
        s_xm = sem("xm_ready")
        s_t4 = sem("xm_transposed")
        s_xhi = sem("xm_hi_ready")
        s_xlo = sem("xm_lo_ready")
        s_log = sem("logits_done")
        s_logc = sem("logits_copied")
        s_logt = sem("logits_transposed")
        s_gap = sem("gap_ready")
        s_tanh = sem("tanh_ready")
        s_comb = sem("comb_ready")
        s_ct = sem("comb_transposed")
        s_mup = sem("expert_up_done")
        s_gelu = sem("gelu_done")
        s_mdn = sem("expert_down_done")
        s_acc = sem("expert_added")
        s_so = sem("expert_vector_order")
        R = BATCHES

        block = ctx.enter_context(nc.Block())

        def at(t, b, n=TPB):
            return t[:, bass.ds(b * n, n), :]

        def later(i, than):
            return not isinstance(i, int) or i > than

        def cols_of(t, b, start=0, size=LENGTH):
            return t[:, bass.ds(b * LENGTH + start, size)]

        @block.sync
        def _(sp):
            sp.dma_start(par[:, :], cols).then_inc(s_par, 16)
            sp.sem_inc(s_store, 16)
            sp.dma_start(at(resid, 0), x_dram[0, :, :, :]).then_inc(s_x, 16)
            sp.wait_ge(s_x, 16)
            for dst, src in ((w1_sb[:, :], w1), (w2_sb[:, :, :], w2.rearrange("(c p) d -> p c d", p=128)),
                             (b2_all[:, 0, :], b2.partition_broadcast(128)),
                             (router_sb[:, :], router), (mb2_sb[:, :], mb2)):
                sp.dma_start(dst, src).then_inc(s_w, 16)
            with sp.Fori(1, BATCHES) as b:
                sp.wait_ge(s_x, b * 16)
                sp.dma_start(at(resid, b), x_dram[bass.ds(b, 1), :, :, :].rearrange("a p j d -> (a p) j d"))\
                    .then_inc(s_x, 16)
            sp.dma_start(mw1_sb[:, :], mw1).then_inc(s_mw, 16)
            sp.dma_start(mw2_sb[:, :, :], mw2.rearrange("e (c p) d -> p (e c) d", p=128)).then_inc(s_mw, 16)
            with sp.Fori(0, BATCHES) as n:
                sp.wait_ge(s_acc, n * EXPERTS + (R + EXPERTS))
                sp.dma_start(out_dram[bass.ds(n, 1), :, :, :].rearrange("a p j d -> (a p) j d"), acc[:, :, :])\
                    .then_inc(s_store, 16)
            sp.wait_ge(s_store, 16 * BATCHES + 16)

        @block.gpsimd
        def _(pool):
            g = nc.gpsimd

            def take_wait():
                g.tensor_tensor(spare_p[:, :], neg_one[:, 0:1], neg_one[:, 0:1], ALU.mult)
            g.memset(ident[:, :], 0.0).then_inc(s_pc, 1)
            g.memset(half_pow[:, :], 0.5)
            g.memset(neg_half[:, :], -0.5)
            g.memset(eps[:, :], EPS)
            g.memset(neg_one[:, :], -1.0).then_inc(s_pc, 1)
            pool.wait_ge(s_pc, 2)
            g.affine_select(out=ident[:, :], in_=ident[:, :], compare_op=ALU.not_equal, fill=1.0, base=0,
                            pattern=[[-1, 128]], channel_multiplier=1).then_inc(s_ident, 1)
            pool.wait_ge(s_par, 16)
            g.tensor_tensor(cst[:, 0:2], par[:, P_RE:P_RE + 2], par[:, P_RE:P_RE + 2], ALU.mult).then_inc(s_pc, 1)
            pool.wait_ge(s_pc, 3)
            g.tensor_tensor(cst[:, 2:3], cst[:, 0:1], cst[:, 1:2], ALU.add).then_inc(s_pc, 1)
            pool.wait_ge(s_pc, 4)
            g.tensor_tensor(cst[:, 3:4], cst[:, 2:3], half_pow[:, 0:1], ALU.pow).then_inc(s_mag, 1)

            def conv_in(b, part, table, done_sem):
                g.tensor_tensor(part[:, :], u[:, :], table[:, :], ALU.mult).then_inc(done_sem, 1)

            def emit(i, post, prep, ahead, base):
                ticks = 0

                def then(ins):
                    nonlocal ticks
                    ins.then_inc(s_po, 1)
                    ticks += 1
                    pool.wait_ge(s_po, base + ticks)
                if prep:
                    pool.wait_ge(s_u, i + 2)
                    conv_in(i + 1, vr, in_re, s_ur)
                if post:
                    pool.wait_ge(s_x2m, i)
                    then(g.tensor_tensor(tmp[:, 0, :], mom2[:, :, 1], eps[:, :], ALU.add))
                    g.tensor_tensor(scale2[:, :], tmp[:, 0, :], neg_half[:, :], ALU.pow).then_inc(s_sc2, 1)
                if prep:
                    conv_in(i + 1, vi, in_im, s_ui)
                    pool.wait_ge(s_vi, i + 2)
                    g.tensor_tensor(vi[:, :], vi[:, :], out_im[:, :], ALU.mult).then_inc(s_ti, 1)
                    pool.wait_ge(s_x1m, i + 2)
                    g.tensor_tensor(negmean1[:, :], mom1[:, :, 0], neg_one[:, :], ALU.mult)
                    then(g.tensor_tensor(tmp[:, 0, :], mom1[:, :, 1], eps[:, :], ALU.add))
                    then(g.tensor_tensor(scale1[:, :], tmp[:, 0, :], neg_half[:, :], ALU.pow))
                    g.tensor_tensor(shift1[:, :], negmean1[:, :], scale1[:, :], ALU.mult).then_inc(s_sc1, 1)
                if ahead:
                    pool.wait_ge(s_x0m, i + 3)
                    var = mom0[:, :, 1]
                    then(g.tensor_tensor(tmp[:, 0, :], var, eps[:, :], ALU.add))
                    then(g.tensor_tensor(tmp[:, 1, :], tmp[:, 0, :], neg_one[:, :], ALU.pow))
                    then(g.tensor_tensor(tmp[:, 1, :], tmp[:, 1, :], var, ALU.mult))
                    then(g.tensor_tensor(tmp[:, 1, :], tmp[:, 1, :], eps[:, :], ALU.add))
                    g.tensor_tensor(tmp[:, 2, :], tmp[:, 1, :], neg_half[:, :], ALU.pow)
                    g.tensor_tensor(unscale0[:, :], tmp[:, 1, :], half_pow[:, :], ALU.pow)
                    then(g.tensor_tensor(tmp[:, 3, :], tmp[:, 0, :], neg_half[:, :], ALU.pow))
                    g.tensor_tensor(scale0[:, :], tmp[:, 2, :], tmp[:, 3, :], ALU.mult).then_inc(s_sc0, 1)
                if prep:
                    r = at(resid, i + 1)
                    pool.wait_ge(s_x1, i + 2)
                    take_wait()
                    then(g.tensor_tensor(r, r, x1[:, :, :], ALU.add))
                    take_wait()
                    g.tensor_tensor(r, r, b2_all[:, :, :].to_broadcast([128, TPB, D]), ALU.add).then_inc(s_base, 1)
                return ticks

            base = 0
            base += emit(-2, False, False, True, base)
            pool.wait_ge(s_tab, 1)
            pool.wait_ge(s_w, 16 * 5)
            base += emit(-1, False, True, True, base)
            base += emit(0, False, True, True, base)
            whole = 1 + 2 + 5 + 1
            with pool.Fori(1, BATCHES - 2) as i:
                n = emit(i, True, True, True, (i - 1) * whole + base)
                assert n == whole
            base += whole * (BATCHES - 3)
            base += emit(BATCHES - 2, True, True, False, base)
            base += emit(BATCHES - 1, True, False, False, base)
            emit(BATCHES, True, False, False, base)

        @block.scalar
        def _(a):
            s = nc.scalar
            a.wait_ge(s_par, 16)

            def emit(i, post, mlp, prep):
                if prep:
                    a.wait_ge(s_t1, i + 2)
                    if later(i, -1):
                        a.wait_ge(s_conv, i + 1)
                        a.wait_ge(s_t2, i + 1)
                    s.activation(u[:, :], trans_p[:, :], ACT.Identity, bias=par[:, BETA:BETA + 1],
                                 scale=par[:, GAMMA:GAMMA + 1]).then_inc(s_u, 1)

                def silu(c):
                    a.wait_ge(s_up, i * FC + c + 1)
                    if c >= 2 or later(i, 0):
                        a.wait_ge(s_dn, i * FC + c - 1)
                    s.activation(act[0][c % 2][:, :], up_p[c % 2][:, :], ACT.Silu,
                                 bias=b1_all[:, c:c + 1]).then_inc(s_silu, 1)
                if mlp:
                    silu(0)
                    silu(1)
                if post:
                    a.wait_ge(s_t4, i)
                    s.activation(cols_of(xm_hi, i - 1), trans_p[:, :], ACT.Copy).then_inc(s_xhi, 1)
                if mlp:
                    silu(2)
                    silu(3)
                if prep:
                    a.wait_ge(s_sc1, i + 2)
                    for j in range(TPB):
                        last = s.activation(h2[:, j, :], x1[:, j, :], ACT.Identity, bias=shift1[:, j:j + 1],
                                            scale=scale1[:, j:j + 1])
                    last.then_inc(s_h2, 1)
                    a.wait_ge(s_t3, i + 2)
                    s.activation(h_hi[:, :], trans_p[:, :], ACT.Copy).then_inc(s_hi, 1)

            emit(-1, False, False, True)
            a.wait_ge(s_b1, 1)
            emit(0, False, True, True)
            with a.Fori(1, BATCHES - 1) as i:
                emit(i, True, True, True)
            emit(BATCHES - 1, True, True, False)
            emit(BATCHES, True, False, False)

            for n in range(BATCHES):
                a.wait_ge(s_log, n + 1)
                if n >= 2:
                    a.wait_ge(s_logt, n - 1)
                s.activation(logit_t[n % 2], up_p[n % 2][0:EXPERTS, :], ACT.Copy).then_inc(s_logc, 1)
            a.wait_ge(s_gap, 1)
            s.activation(th[:, :, :], pick[:, :, :], ACT.Tanh, scale=0.5).then_inc(s_tanh, 1)
            for n in range(BATCHES):
                a.wait_ge(s_ct, n + 1)
                if n >= 2:
                    a.wait_ge(s_mdn, n - 1)
                s.activation(comb_t[n % 2], up_p[n % 2][0:EXPERTS, :], ACT.Copy).then_inc(s_gelu, 1)

            def experts(n):
                for e in range(EXPERTS):
                    for c in range(EC):
                        a.wait_ge(s_mup, n * (EXPERTS * EC) + (e * EC + c + 1))
                        if c == 0:
                            a.wait_ge(s_mdn, n * EXPERTS + (R + e - 1))
                        s.activation(act[e % 2][c][:, :], up_p[c][:, :], ACT.Gelu,
                                     bias=par[:, MB1 + e * EC + c:MB1 + e * EC + c + 1]).then_inc(s_gelu, 1)
            with a.Fori(0, BATCHES) as n:
                experts(n)

        @block.tensor
        def _(pe):
            t = nc.tensor

            def transposed(src, dst, done):
                for j in range(TPB):
                    last = t.transpose(dst[:, j * TILE:(j + 1) * TILE], src(j), ident[:, :])
                last.then_inc(done, 1)

            def up(dst, hi, lo, w_hi, w_lo, done):
                for h in range(LENGTH // HALF):
                    d = dst[:, h * HALF:(h + 1) * HALF]
                    t.matmul(d, w_hi, lo(h), start=True, stop=False)
                    t.matmul(d, w_hi, hi(h), start=False, stop=False)
                    last = t.matmul(d, w_lo, hi(h), start=False, stop=True)
                last.then_inc(done, 1)

            def down(dst, hid, w, first_chunk, last_chunk, done=None):
                per_bank = HALF // D
                for j in range(TPB):
                    last = t.matmul(dst[:, j * D:(j + 1) * D], hid[:, j * TILE:(j + 1) * TILE], w,
                                    start=first_chunk and j % per_bank == 0, stop=last_chunk,
                                    skip_group_check=True)
                if done is not None:
                    last.then_inc(done, 1)

            def attn_up(i, c):
                if c >= 2 or later(i, 0):
                    pe.wait_ge(s_silu, i * FC + c - 1)
                up(up_p[c % 2], lambda h: h_hi[:, h * HALF:(h + 1) * HALF], lambda h: h_lo[:, h * HALF:(h + 1) * HALF],
                   w1_hi[:, c * 128:(c + 1) * 128], w1_lo[:, c * 128:(c + 1) * 128], s_up)

            def attn_down(i, c):
                pe.wait_ge(s_silu, i * FC + c + 1)
                if c == 0:
                    pe.wait_ge(s_x2, i)
                down(down_p, act[0][c % 2], w2_sb[:, c, :], c == 0, c == FC - 1, s_dn)

            def emit(i, post, mlp, prep):
                if prep:
                    pe.wait_ge(s_hn, i + 2)
                    if later(i, -1):
                        pe.wait_ge(s_lo, i + 1)
                    transposed(lambda j: hn[:, j, :], trans_p, s_t1)
                if mlp:
                    pe.wait_ge(s_lo, i + 1)
                    attn_up(i, 0)
                    attn_up(i, 1)
                    attn_down(i, 0)
                if post:
                    pe.wait_ge(s_xm, i)
                    if prep:
                        pe.wait_ge(s_u, i + 2)
                    else:
                        pe.wait_ge(s_lo, BATCHES)
                        if i == BATCHES:
                            pe.wait_ge(s_xlo, i - 1)
                    transposed(lambda j: act_xm[:, j, :], trans_p, s_t4)
                if mlp:
                    attn_up(i, 2)
                    attn_down(i, 1)
                if prep:
                    pe.wait_ge(s_conv, i + 2)
                    if post:
                        pe.wait_ge(s_xlo, i)
                    transposed(lambda j: u[:, j * TILE:(j + 1) * TILE], trans_p, s_t2)
                if mlp:
                    attn_up(i, 3)
                    attn_down(i, 2)
                    attn_down(i, 3)
                if prep:
                    pe.wait_ge(s_h2, i + 2)
                    pe.wait_ge(s_x1, i + 2)
                    transposed(lambda j: h2[:, j, :], trans_p, s_t3)

            pe.wait_ge(s_ident, 1)
            pe.wait_ge(s_w, 16 * 5)
            pe.wait_ge(s_par, 16)
            for c in range(FC):
                last = t.matmul(down_p[:, c:c + 1], w1_sb[:, c * 128:(c + 1) * 128], par[:, BETA:BETA + 1],
                                start=True, stop=True)
            last.then_inc(s_b1raw, 1)
            emit(-1, False, False, True)
            pe.wait_ge(s_wsplit, 1)
            pe.wait_ge(s_b1, 1)
            emit(0, False, True, True)
            with pe.Fori(1, BATCHES - 1) as i:
                emit(i, True, True, True)
            emit(BATCHES - 1, True, True, False)
            emit(BATCHES, True, False, False)

            pe.wait_ge(s_xlo, BATCHES)
            pe.wait_ge(s_wsplit, 2)

            def logits_turned(n):
                pe.wait_ge(s_logc, n + 1)
                for j in range(TPB):
                    k = (n * TPB + j) * EXPERTS
                    last = t.transpose(trans_p[:, k:k + EXPERTS], logit_t[n % 2][:, j * TILE:(j + 1) * TILE],
                                       ident[0:EXPERTS, 0:EXPERTS])
                last.then_inc(s_logt, 1)
            for n in range(BATCHES):
                if n >= 2:
                    pe.wait_ge(s_logc, n - 1)
                up(up_p[n % 2], lambda h: cols_of(xm_hi, n, h * HALF, HALF), lambda h: cols_of(xm_lo, n, h * HALF, HALF),
                   router_hi[:, :], router_lo[:, :], s_log)
                if n >= 1:
                    logits_turned(n - 1)
            logits_turned(BATCHES - 1)

            def comb_turned(n):
                if n >= 2:
                    pe.wait_ge(s_gelu, n - 1)
                for j in range(TPB):
                    last = t.matmul(up_p[n % 2][0:EXPERTS, j * TILE:(j + 1) * TILE], comb[:, n * TPB + j, :],
                                    ident[:, :], start=True, stop=True)
                last.then_inc(s_ct, 1)

            def last_bias(n):
                pe.wait_ge(s_gelu, n + 1)
                if n >= 2:
                    pe.wait_ge(s_acc, n - 1)
                for j in range(TPB):
                    last = t.matmul(moe_p[n % 2][:, j * D:(j + 1) * D], comb_t[n % 2][:, j * TILE:(j + 1) * TILE],
                                    mb2_sb[:, :], start=True, stop=True)
                last.then_inc(s_mdn, 1)
            pe.wait_ge(s_comb, 1)
            for n in range(BATCHES):
                comb_turned(n)
                if n >= 1:
                    last_bias(n - 1)
            last_bias(BATCHES - 1)

            def expert_up(n, e):
                for c in range(EC):
                    pe.wait_ge(s_gelu, n * (EXPERTS * EC) + (R + (e - 1) * EC + c + 1))
                    k = (e * EC + c) * 128
                    up(up_p[c], lambda h: cols_of(xm_hi, n, h * HALF, HALF),
                       lambda h: cols_of(xm_lo, n, h * HALF, HALF), mw1_hi[:, k:k + 128], mw1_lo[:, k:k + 128], s_mup)

            def expert_down(n, e):
                pe.wait_ge(s_acc, n * EXPERTS + (R + e - 1))
                for c in range(EC):
                    pe.wait_ge(s_gelu, n * (EXPERTS * EC) + (R + e * EC + c + 1))
                    down(moe_p[e % 2], act[e % 2][c], mw2_sb[:, e * EC + c, :], c == 0, c == EC - 1,
                         s_mdn if c == EC - 1 else None)
            expert_up(0, 0)

            def experts(n, more):
                for e in range(EXPERTS):
                    if e + 1 < EXPERTS:
                        expert_up(n, e + 1)
                    elif more:
                        expert_up(n + 1, 0)
                    expert_down(n, e)
            with pe.Fori(0, BATCHES - 1) as n:
                experts(n, True)
            experts(BATCHES - 1, False)

        @block.vector
        def _(v):
            d = nc.vector
            made = [0]

            def take_wait():
                d.memset(spare_v[:, :], 0.0)

            def link(ins):
                made[0] += 1
                ins.then_inc(s_vc, 1)
                v.wait_ge(s_vc, made[0])

            def moments(b, src, mom, base, ticks, done):
                take_wait()
                for j in range(TPB):
                    last = d.bn_stats(stats[:, j, :], src(j))
                last.then_inc(s_vo, 1)
                v.wait_ge(s_vo, base + ticks)
                take_wait()
                for j in range(TPB):
                    last = d.bn_aggr(mom[:, j, :], stats[:, j, :])
                last.then_inc(done, 1)

            def tile(b, j):
                return resid[:, bass.ds(b * TPB + j, 1), :].rearrange("p a d -> p (a d)")

            def x0_norm(b, base):
                v.wait_ge(s_x, b * 16 + 16)
                moments(b, lambda j: tile(b, j), mom0, base, 1, s_x0m)
                v.wait_ge(s_sc0, b + 1)
                v.wait_ge(s_x0m, b + 1)
                if later(b, 0):
                    v.wait_ge(s_t1, b)
                for j in range(TPB):
                    last = d.tensor_scalar(hn[:, j, :], tile(b, j), mom0[:, j, 0:1], scale0[:, j:j + 1],
                                           ALU.subtract, ALU.mult)
                last.then_inc(s_hn, 1)
                return 1

            def emit(i, post, prep, ahead, base):
                ticks = 0

                def then(ins):
                    nonlocal ticks
                    ins.then_inc(s_vo, 1)
                    ticks += 1
                    v.wait_ge(s_vo, base + ticks)
                if post:
                    v.wait_ge(s_dn, i * FC)
                    v.wait_ge(s_base, i)
                    r = at(resid, i - 1)
                    d.tensor_tensor(r, down_p[:, :].rearrange("p (j d) -> p j d", d=D), r, ALU.add).then_inc(s_x2, 1)
                    v.wait_ge(s_x2, i)
                    ticks += 1
                    moments(i - 1, lambda j: tile(i - 1, j), mom2, base, ticks, s_x2m)
                if prep:
                    decay = decay_c.to_broadcast([128, LENGTH])
                    v.wait_ge(s_ur, i + 2)
                    then(d.tensor_tensor_scan(vr[:, :], decay, vr[:, :], v0_re, ALU.mult, ALU.add))
                    v.wait_ge(s_ui, i + 2)
                    d.tensor_tensor_scan(vi[:, :], decay, vi[:, :], v0_im, ALU.mult, ALU.add).then_inc(s_vi, 1)
                    then(d.tensor_tensor(vr[:, :], vr[:, :], out_re[:, :], ALU.mult))
                if post:
                    v.wait_ge(s_sc2, i)
                    v.wait_ge(s_x2m, i)
                    if later(i, 1):
                        v.wait_ge(s_t4, i - 1)
                    for j in range(TPB):
                        last = d.tensor_scalar(act_xm[:, j, :], tile(i - 1, j), mom2[:, j, 0:1], scale2[:, j:j + 1],
                                               ALU.subtract, ALU.mult)
                    last.then_inc(s_xm, 1)
                if prep:
                    v.wait_ge(s_ti, i + 2)
                    d.tensor_tensor(u[:, :], vr[:, :], vi[:, :], ALU.subtract).then_inc(s_conv, 1)
                if post:
                    v.wait_ge(s_xhi, i)
                    d.tensor_tensor(cols_of(xm_lo, i - 1), trans_p[:, :], cols_of(xm_hi, i - 1).bitcast(f32),
                                    ALU.subtract).then_inc(s_xlo, 1)
                if prep:
                    v.wait_ge(s_t2, i + 2)
                    if later(i, -1):
                        v.wait_ge(s_base, i + 1)
                    for j in range(TPB):
                        last = d.scalar_tensor_tensor(out=x1[:, j, :], in0=hn[:, j, :], scalar=unscale0[:, j:j + 1],
                                                      in1=trans_p[:, j * D:(j + 1) * D], op0=ALU.mult, op1=ALU.add)
                    last.then_inc(s_x1, 1)
                    v.wait_ge(s_x1, i + 2)
                    ticks += 1
                    moments(i + 1, lambda j: x1[:, j, :], mom1, base, ticks, s_x1m)
                if ahead:
                    ticks += 1
                    b = i + 2
                    v.wait_ge(s_x, b * 16 + 16)
                    v.wait_ge(s_x1m, b)
                    moments(b, lambda j: tile(b, j), mom0, base, ticks, s_x0m)
                    v.wait_ge(s_sc0, b + 1)
                    v.wait_ge(s_x0m, b + 1)
                    v.wait_ge(s_t1, b)
                    for j in range(TPB):
                        last = d.tensor_scalar(hn[:, j, :], tile(b, j), mom0[:, j, 0:1], scale0[:, j:j + 1],
                                               ALU.subtract, ALU.mult)
                    last.then_inc(s_hn, 1)
                if prep:
                    v.wait_ge(s_hi, i + 2)
                    d.tensor_tensor(h_lo[:, :], trans_p[:, :], h_hi[:, :].bitcast(f32), ALU.subtract).then_inc(s_lo, 1)
                return ticks

            base = x0_norm(0, 0)

            v.wait_ge(s_par, 16)
            v.wait_ge(s_mag, 1)
            mag = cst[:, 3:4]
            link(d.tensor_scalar(cst[:, 4:5], mag, EXP_LARGEST, -1.0 / 2 ** EXP_HALVINGS, ALU.min, ALU.mult))
            link(d.reciprocal(cst[:, 5:6], mag))
            for k in range(EXP_DEGREE):
                last = d.tensor_scalar(yk[:, k:k + 1], cst[:, 4:5], 1.0 / (k + 1), None, ALU.mult)
            link(last)
            link(d.tensor_scalar(cst[:, 6:7], yk[:, EXP_DEGREE - 1:EXP_DEGREE], 1.0, None, ALU.add))
            for k in reversed(range(1, EXP_DEGREE - 1)):
                link(d.tensor_scalar(cst[:, 6:7], cst[:, 6:7], yk[:, k:k + 1], 1.0, ALU.mult, ALU.add))
            link(d.tensor_scalar(cst[:, 6:7], cst[:, 6:7], yk[:, 0:1], None, ALU.mult))
            for _ in range(EXP_HALVINGS):
                link(d.scalar_tensor_tensor(out=cst[:, 6:7], in0=cst[:, 6:7], scalar=2.0, in1=cst[:, 6:7],
                                            op0=ALU.add, op1=ALU.mult))
            link(d.tensor_scalar(cst[:, 7:8], cst[:, 6:7], 1.0, None, ALU.add))
            decay_c = cst[:, 7:8]
            z = [(cst[:, 8:9], cst[:, 9:10]), (cst[:, 10:11], cst[:, 11:12])]
            link(d.tensor_scalar(cst[:, 8:10], par[:, P_RE:P_RE + 2], cst[:, 5:6], None, ALU.mult))
            v0 = cst[:, 16:18]
            link(d.tensor_scalar(v0, par[:, LAST_RE:LAST_RE + 2], z[0][0], None, ALU.mult))
            link(d.tensor_scalar(cst[:, 18:20], par[:, LAST_RE:LAST_RE + 2], z[0][1], None, ALU.mult))
            link(d.tensor_tensor(cst[:, 16:17], cst[:, 16:17], cst[:, 19:20], ALU.subtract))
            link(d.tensor_tensor(cst[:, 17:18], cst[:, 17:18], cst[:, 18:19], ALU.add))
            v0_re, v0_im = cst[:, 16:17], cst[:, 17:18]
            d.memset(out_re[:, 0:1], 1.0)
            link(d.memset(out_im[:, 0:1], 0.0))
            n, k = 1, 0
            while n < LENGTH:
                (zr, zi), (nr, ni) = z[k], z[1 - k]
                d.tensor_scalar(in_re[:, 0:n], out_im[:, 0:n], zi, None, ALU.mult)
                d.tensor_scalar(in_im[:, 0:n], out_re[:, 0:n], zi, None, ALU.mult)
                d.tensor_tensor(cst[:, 12:13], zi, zi, ALU.mult)
                link(d.tensor_tensor(cst[:, 13:14], zr, zi, ALU.mult))
                d.scalar_tensor_tensor(out=out_re[:, n:2 * n], in0=out_re[:, 0:n], scalar=zr, in1=in_re[:, 0:n],
                                       op0=ALU.mult, op1=ALU.subtract)
                d.scalar_tensor_tensor(out=out_im[:, n:2 * n], in0=out_im[:, 0:n], scalar=zr, in1=in_im[:, 0:n],
                                       op0=ALU.mult, op1=ALU.add)
                d.tensor_scalar(ni, cst[:, 13:14], 2.0, None, ALU.mult)
                link(d.scalar_tensor_tensor(out=nr, in0=zr, scalar=zr, in1=cst[:, 12:13], op0=ALU.mult,
                                            op1=ALU.subtract))
                both = cst[:, 8:10] if k else cst[:, 10:12]
                link(d.tensor_tensor(cst[:, 12:14], both, both, ALU.mult))
                link(d.tensor_tensor(cst[:, 14:15], cst[:, 12:13], cst[:, 13:14], ALU.add))
                link(d.tensor_scalar(cst[:, 14:15], cst[:, 14:15], -0.5, 1.5, ALU.mult, ALU.add))
                link(d.tensor_scalar(both, both, cst[:, 14:15], None, ALU.mult))
                n, k = 2 * n, 1 - k
            i_re, i_im = par[:, INIT_RE:INIT_RE + 1], par[:, INIT_IM:INIT_IM + 1]
            d.tensor_scalar(in_re[:, :], out_im[:, :], i_im, None, ALU.mult)
            link(d.tensor_scalar(in_im[:, :], out_im[:, :], i_re, None, ALU.mult))
            d.scalar_tensor_tensor(out=in_re[:, :], in0=out_re[:, :], scalar=i_re, in1=in_re[:, :],
                                   op0=ALU.mult, op1=ALU.add)
            d.scalar_tensor_tensor(out=in_im[:, :], in0=out_re[:, :], scalar=i_im, in1=in_im[:, :],
                                   op0=ALU.mult, op1=ALU.subtract).then_inc(s_tab, 1)

            v.wait_ge(s_w, 16 * 5)
            gam = par[:, GAMMA:GAMMA + 1]
            link(d.tensor_scalar(act[0][0][:, 0:FF], w1_sb[:, :], gam, None, ALU.mult))
            link(d.tensor_copy(w1_hi[:, :], act[0][0][:, 0:FF]))
            d.tensor_tensor(w1_lo[:, :], act[0][0][:, 0:FF], w1_hi[:, :].bitcast(f32), ALU.subtract)\
                .then_inc(s_wsplit, 1)
            v.wait_ge(s_b1raw, 1)
            d.tensor_tensor(b1_all[:, :], down_p[:, 0:FC], par[:, B1:B1 + FC], ALU.add).then_inc(s_b1, 1)

            base += emit(-1, False, True, True, base)
            base += emit(0, False, True, True, base)
            whole = 1 + 2 + 1 + 1
            with v.Fori(1, BATCHES - 2) as i:
                n = emit(i, True, True, True, (i - 1) * whole + base)
                assert n == whole, n
            base += whole * (BATCHES - 3)
            base += emit(BATCHES - 2, True, True, False, base)
            v.wait_ge(s_mw, 16 * 2)
            d.memset(router_hi[:, :].bitcast(f32), 0.0)
            link(d.memset(router_lo[:, :].bitcast(f32), 0.0))
            d.tensor_copy(router_hi[:, 0:EXPERTS], router_sb[:, :])
            link(d.tensor_copy(mw1_hi[:, :], mw1_sb[:, :]))
            d.tensor_tensor(router_lo[:, 0:EXPERTS], router_sb[:, :], router_hi[:, 0:EXPERTS].bitcast(f32), ALU.subtract)
            d.tensor_tensor(mw1_lo[:, :], mw1_sb[:, :], mw1_hi[:, :].bitcast(f32), ALU.subtract).then_inc(s_wsplit, 1)
            for e in range(EXPERTS):
                last = d.memset(rank[:, :, e:e + 1], float(EXPERTS - e))
            link(last)
            base += emit(BATCHES - 1, True, False, False, base)
            emit(BATCHES, True, False, False, base)

            def wide(t1):
                return t1.to_broadcast([128, TILES, EXPERTS])
            v.wait_ge(s_logt, BATCHES)
            link(d.tensor_copy(logits, trans_p[:, 0:TILES * EXPERTS].rearrange("p (t e) -> p t e", e=EXPERTS)))

            def choose(values, top, onehot):
                link(d.tensor_reduce(top[:, :, :], values, AX, ALU.max))
                link(d.tensor_tensor(scored, values, wide(top[:, :, :]), ALU.is_equal))
                link(d.tensor_tensor(scored, scored, rank[:, :, :].to_broadcast([128, TILES, EXPERTS]), ALU.mult))
                link(d.tensor_reduce(pick[:, :, :], scored, AX, ALU.max))
                link(d.tensor_tensor(onehot, scored, wide(pick[:, :, :]), ALU.is_equal))
            choose(logits, best, first)
            link(d.scalar_tensor_tensor(out=logits, in0=first, scalar=-LARGE, in1=logits, op0=ALU.mult, op1=ALU.add))
            choose(logits, runner, second)
            d.tensor_tensor(pick[:, :, :], best[:, :, :], runner[:, :, :], ALU.subtract).then_inc(s_gap, 1)
            v.wait_ge(s_tanh, 1)
            d.tensor_scalar(prob1[:, :, :], th[:, :, :], 0.5, 0.5, ALU.mult, ALU.add)
            link(d.tensor_scalar(prob2[:, :, :], th[:, :, :], -0.5, 0.5, ALU.mult, ALU.add))
            d.tensor_tensor(first, first, wide(prob1[:, :, :]), ALU.mult)
            link(d.tensor_tensor(second, second, wide(prob2[:, :, :]), ALU.mult))
            link(d.tensor_tensor(comb, first, second, ALU.add))
            v.sem_inc(s_comb, 1)

            for n in range(BATCHES):
                v.wait_ge(s_mdn, n + 1)
                r = at(resid, n)
                d.tensor_tensor(r, moe_p[n % 2][:, :].rearrange("p (j d) -> p j d", d=D), r, ALU.add)\
                    .then_inc(s_acc, 1)

            with v.Fori(0, BATCHES) as n:
                v.wait_ge(s_acc, n * EXPERTS + R)
                d.tensor_copy(comb_n[:, :, :], comb_buf[:, bass.ds(n * TPB, TPB), :]).then_inc(s_so, 1)
                v.wait_ge(s_so, n + 1)
                for e in range(EXPERTS):
                    v.wait_ge(s_mdn, n * EXPERTS + (R + e + 1))
                    if e == 0:
                        v.wait_ge(s_store, n * 16 + 16)
                    else:
                        v.wait_ge(s_acc, n * EXPERTS + (R + e))
                    for j in range(TPB):
                        last = d.scalar_tensor_tensor(
                            out=acc[:, j, :], in0=moe_p[e % 2][:, j * D:(j + 1) * D], scalar=comb_n[:, j, e:e + 1],
                            in1=tile(n, j) if e == 0 else acc[:, j, :], op0=ALU.mult, op1=ALU.add)
                    last.then_inc(s_acc, 1)


def kernel(**inputs):
    import numpy as np
    import concourse.bacc as bacc
    from concourse.bass_utils import run_bass_kernel_spmd

    p = {k: np.asarray(v) for k, v in inputs.items()}
    a, f = "L0_attn_", "L0_ffn_"
    columns = [p[a + k][:, None] for k in ("ln_gamma", "ln_beta", "phazor_re", "phazor_im", "phazor_init_re",
                                           "phazor_init_im", "last_conv_re", "last_conv_im")]
    columns.append(p[a + "b1"].reshape(FC, 128).T)
    columns.append(p[f + "b1"].reshape(EXPERTS * EC, 128).T)
    arrays = {
        "x": p[a + "x"],
        "cols": np.concatenate(columns, axis=1),
        "w1": p[a + "w1"],
        "w2": p[a + "w2"],
        "b2": p[a + "b2"],
        "router": p[f + "router_w"].T,
        "mw1": p[f + "w1"].reshape(EXPERTS * EF, D).T,
        "mw2": p[f + "w2"].transpose(0, 2, 1),
        "mb2": p[f + "b2"],
    }
    arrays = {f"in_{k}": np.ascontiguousarray(v) for k, v in arrays.items()}
    nc = bacc.Bacc("TRN2", target_bir_lowering=False, num_devices=1)
    args = [nc.dram_tensor(k, v.shape, mybir.dt.from_np(v.dtype), kind="ExternalInput").ap()
            for k, v in arrays.items()]
    args.append(nc.dram_tensor("out", (BATCHES, LENGTH, D), mybir.dt.float32, kind="ExternalOutput").ap())
    block_moe_kernel(nc, *args)
    return run_bass_kernel_spmd(nc, [arrays], core_ids=[0]).results[0]["out"]
```

```python
import concourse.bass as bass
from concourse import mybir
from contextlib import ExitStack

BATCHES, LENGTH, D = 8, 1024, 128
FF = 512
EXPERTS, EF = 8, 256
TILE = 128
TPB = LENGTH // TILE
TILES = BATCHES * TPB
HALF = 512
FC = FF // 128
EC = EF // 128
EPS = 1e-5
(GAMMA, BETA, P_RE, P_IM, INIT_RE, INIT_IM, LAST_RE, LAST_IM) = range(8)
B1 = 8
MB1 = B1 + FC
MB2 = MB1 + EXPERTS * EC
COLS = MB2 + EXPERTS
EXP_HALVINGS = 7
EXP_DEGREE = 10
EXP_LARGEST = 104.0
LARGE = 3.0e38
STEP = 32
POWERS = 10
SPARE = 8


def block_moe_kernel(nc, x, cols, w1, w2, b2, router, mw1, mw2, out):
    f32 = mybir.dt.float32
    f32r = mybir.dt.float32r
    ALU = mybir.AluOpType
    ACT = mybir.ActivationFunctionType
    AX = mybir.AxisListType.X

    x_dram = x.rearrange("b (j p) d -> b p j d", p=TILE)
    out_dram = out.rearrange("b (j p) d -> b p j d", p=TILE)

    ctx = ExitStack()
    with ctx:
        def sb(name, shape, dt=f32):
            return ctx.enter_context(nc.sbuf_tensor(name, shape, dt))

        def sem(name):
            return ctx.enter_context(nc.semaphore(name))

        resid = sb("resid", [128, TILES, D])
        par = sb("par", [128, COLS])
        w1_hi = sb("w1_hi", [128, FF], f32r)
        w1_lo = sb("w1_lo", [128, FF], f32r)
        w2_sb = sb("w2_sb", [128, FC, D])
        b1_all = sb("b1_all", [128, FC])
        b2_hi_lo = sb("b2_hi_lo", [2, HALF], f32r)
        ones = sb("ones", [2, 128], f32r)
        mw1_hi = sb("mw1_hi", [128, EXPERTS * EF], f32r)
        mw1_lo = sb("mw1_lo", [128, EXPERTS * EF], f32r)
        mw2_hi = sb("mw2_hi", [128, EXPERTS * EC * D], f32r)
        mw2_lo = sb("mw2_lo", [128, EXPERTS * EC * D], f32r)
        router_sb = sb("router_sb", [128, EXPERTS])
        router_hi = sb("router_hi", [128, 128], f32r)
        router_lo = sb("router_lo", [128, 128], f32r)
        ident = sb("ident", [128, 128])
        rank = sb("rank", [128, 1, EXPERTS])
        hid_hi = [[sb(f"hid_hi{c}{q}", [128, LENGTH], f32r) for q in range(2)] for c in range(EC)]
        hid_lo = [[sb(f"hid_lo{c}{q}", [128, LENGTH], f32r) for q in range(2)] for c in range(EC)]
        h_hi, h_lo = hid_hi[0][0], hid_lo[0][0]
        xm_hi = [sb(f"xm_hi{q}", [128, LENGTH], f32r) for q in range(2)]
        xm_lo = [sb(f"xm_lo{q}", [128, LENGTH], f32r) for q in range(2)]
        work = sb("work", [128, 20, LENGTH])

        def slot(k):
            return work[:, k, :]

        def tiled(ap):
            return ap.rearrange("p (j d) -> p j d", d=D)
        in_re, in_im, out_re, out_im = slot(0), slot(1), slot(2), slot(3)
        hn, xn = tiled(slot(4)), tiled(slot(5))
        u, vr, vi = slot(6), slot(7), slot(8)
        x1, h2 = tiled(slot(9)), tiled(slot(10))
        silu = [slot(11), slot(12)]
        mw1_sb = work[:, 13:15, :].rearrange("p a b -> p (a b)")
        mw2_sb = work[:, 15:17, :].rearrange("p a b -> p (a b)")
        b2_rows, b2_lo = work[0:2, 18, 0:HALF], work[0:2, 18, HALF:LENGTH]
        b2_hi = xm_hi[0][0:2, 0:HALF]
        w1_sb, w1_g = work[:, 17, 0:FF], work[:, 17, FF:2 * FF]
        weight = [slot(e) for e in range(EXPERTS)]
        xm = tiled(slot(8))
        total = [slot(9), slot(10)]
        part = [slot(11), slot(12)]
        hid = [[slot(13), slot(14)], [slot(15), slot(16)]]
        result = tiled(slot(17))
        logit_t = work[0:EXPERTS, 18, :]
        comb_t = work[0:EXPERTS, 19, :]
        cst = sb("cst", [128, 32])
        ecs = sb("ecs", [128, 8])
        yk = sb("yk", [128, EXP_DEGREE])
        zz = sb("zz", [128, POWERS, 2])
        sq = sb("sq", [128, 4])
        low_high = sb("low_high", [128, 2, 2, STEP])
        prod = sb("prod", [128, 4, 2, STEP])
        stats0 = sb("stats0", [128, TPB, 6])
        stats1 = sb("stats1", [128, TPB, 6])
        stats2 = sb("stats2", [128, TPB, 6])
        mom0 = sb("mom0", [128, TPB, 2])
        mom1 = sb("mom1", [128, TPB, 2])
        mom2 = sb("mom2", [128, TPB, 2])
        half_pow = sb("half_pow", [128, TPB])
        neg_half = sb("neg_half", [128, 2 * TPB])
        neg_one = sb("neg_one", [128, TPB])
        eps = sb("eps", [128, TPB])
        tmp = sb("tmp", [128, 8, TPB])
        var_eps = sb("var_eps", [128, 2, TPB])
        norm_pow = sb("norm_pow", [128, 2, TPB])
        shift0 = sb("shift0", [128, TPB])
        unscale0 = sb("unscale0", [128, TPB, 1])
        scale1 = sb("scale1", [128, TPB])
        shift1 = sb("shift1", [128, TPB])
        scale2 = sb("scale2", [128, TPB])
        shift2 = sb("shift2", [128, TPB])
        spare_v = sb("spare_v", [128, SPARE])
        spare_p = sb("spare_p", [128, SPARE])
        logits = sb("logits", [128, TPB, EXPERTS])
        first = sb("first", [128, TPB, EXPERTS])
        second = sb("second", [128, TPB, EXPERTS])
        scored = sb("scored", [128, TPB, EXPERTS])
        comb = sb("comb", [128, TPB, EXPERTS])
        best = sb("best", [128, TPB, 1])
        runner = sb("runner", [128, TPB, 1])
        pick = sb("pick", [128, TPB, 1])
        gap = sb("gap", [128, TPB, 1])
        th = sb("th", [128, TPB, 1])
        prob = sb("prob", [128, 2, TPB, 1])
        comb_dram = nc.dram_tensor("comb_weights", (BATCHES, EXPERTS, LENGTH), f32, kind="Internal").ap()

        def pair(name):
            return ctx.enter_context(nc.psum_tensor(name, [128, LENGTH], f32))
        turn_p = pair("turn_p")
        up_p = [pair("up_p0"), pair("up_p1")]
        down_p = pair("down_p")

        s_par = sem("params_loaded")
        s_w = sem("weights_loaded")
        s_mw = sem("expert_weights_loaded")
        s_x = sem("x_loaded")
        s_cd = sem("comb_weights_stored")
        s_cb = [sem(f"comb_weights_spread{e}") for e in range(EXPERTS)]
        s_store = sem("block_stored")
        s_pc = sem("pool_const_order")
        s_vc = sem("vector_const_order")
        s_ident = sem("identity_ready")
        s_mag = sem("magnitude_ready")
        s_decay = sem("decay_ready")
        s_low_high = sem("table_factors_ready")
        s_ore = sem("out_re_ready")
        s_oim = sem("out_im_products_ready")
        s_ire = sem("init_products_ready")
        s_tab = sem("tables_ready")
        s_wsplit = sem("weights_split")
        s_mwhi = sem("expert_weights_high")
        s_b1raw = sem("bias_product_done")
        s_b1 = sem("bias_ready")
        s_po = sem("pool_order")
        s_vo = sem("vector_order")
        s_x0m = sem("x0_moments")
        s_sc0 = sem("x0_scales")
        s_un = sem("x0_unscale")
        s_hn = sem("hn_ready")
        s_xn = sem("xn_ready")
        s_t1 = sem("hn_turned")
        s_u = sem("u_ready")
        s_ui = sem("u_im_ready")
        s_vi = sem("v_im_ready")
        s_ti = sem("out_im_ready")
        s_conv = sem("conv_ready")
        s_t2 = sem("conv_turned")
        s_x1 = sem("x1_ready")
        s_x1m = sem("x1_moments")
        s_sc1 = sem("x1_scales")
        s_h2 = sem("h2_ready")
        s_base = sem("residual_ready")
        s_t3 = sem("h2_turned")
        s_hi = sem("h_hi_ready")
        s_lo = sem("h_lo_ready")
        s_up = sem("up_done")
        s_silu = sem("silu_done")
        s_dn = sem("down_done")
        s_x2 = sem("x2_ready")
        s_x2m = sem("x2_moments")
        s_sc2 = sem("x2_scales")
        s_xm = sem("xm_ready")
        s_t4 = sem("xm_turned")
        s_xhi = sem("xm_hi_ready")
        s_xlo = sem("xm_lo_ready")
        s_rt = sem("router_done")
        s_lt = sem("logits_t_ready")
        s_tn = sem("logits_turned")
        s_lg = sem("logits_ready")
        s_gap = sem("gap_ready")
        s_tanh = sem("tanh_ready")
        s_comb = sem("comb_ready")
        s_cm = sem("comb_turned")
        s_ct = sem("comb_t_ready")
        s_otr = sem("total_turned")
        s_out = sem("result_ready")
        s_last = sem("last_total_ready")
        s_lotr = sem("last_total_turned")
        s_tv = sem("choice_order")
        s_mup = sem("expert_up_done")
        s_gelu = sem("gelu_done")
        s_hi0 = sem("hid_hi0_ready")
        s_hi1 = sem("hid_hi1_ready")
        s_elo = sem("hid_lo_ready")
        s_edn = sem("expert_down_done")
        s_mul = sem("part_ready")
        s_add = sem("part_added")

        block = ctx.enter_context(nc.Block())
        LAST = BATCHES - 1

        def after(eng, semaphore, count):
            if not isinstance(count, int) or count > 0:
                eng.wait_ge(semaphore, count)

        def batch_of(t, b):
            return t[:, bass.ds(b * TPB, TPB), :]

        def tile_of(t, b, j):
            return t[:, bass.ds(b * TPB + j, 1), :].rearrange("p a d -> p (a d)")

        def half(ap, h):
            return ap[:, h * HALF:(h + 1) * HALF]

        fast = [low_high[:, m, 0:1, :].to_broadcast([128, STEP, STEP]) for m in range(2)]
        slow = [low_high[:, m, 1, :].unsqueeze(2).to_broadcast([128, STEP, STEP]) for m in range(2)]

        def grid(ap):
            return ap.rearrange("p (h l) -> p h l", l=STEP)

        def some(h):
            return slice(h * TPB // 2, (h + 1) * TPB // 2)

        def live(b):
            return not isinstance(b, int) or 0 <= b <= LAST

        @block.sync
        def _(sp):
            sp.dma_start(par[:, :], cols).then_inc(s_par, 16)
            sp.dma_start(batch_of(resid, 0), x_dram[0, :, :, :]).then_inc(s_x, 16)
            for dst, src in ((w1_sb, w1), (w2_sb[:, :, :], w2.rearrange("(c p) d -> p c d", p=128)),
                             (b2_rows, b2), (router_sb[:, :], router)):
                sp.dma_start(dst, src).then_inc(s_w, 16)
            sp.dma_start(mw1_sb, mw1).then_inc(s_mw, 16)
            sp.dma_start(tiled(mw2_sb), mw2.rearrange("e (c p) d -> p (e c) d", p=128)).then_inc(s_mw, 16)
            with sp.Fori(1, BATCHES) as b:
                sp.wait_ge(s_x, b * 16)
                sp.dma_start(batch_of(resid, b), x_dram[bass.ds(b, 1), :, :, :].rearrange("a p j d -> (a p) j d"))\
                    .then_inc(s_x, 16)

            def store(n):
                sp.wait_ge(s_out, n + 1)
                sp.dma_start(out_dram[bass.ds(n, 1), :, :, :].rearrange("a p j d -> (a p) j d"), result)\
                    .then_inc(s_store, 16)

            def spread(b):
                sp.wait_ge(s_ct, b + 1)
                rows = comb_dram[bass.ds(b, 1), :, :].rearrange("a e t -> (a e) t")
                sp.dma_start(rows, comb_t).then_inc(s_cd, 16)
                for e in range(EXPERTS):
                    after(sp, s_mul, (b - 1) * (2 * EXPERTS) + (2 * e + 2))
                    if e == 0:
                        after(sp, s_store, (b - 1) * 16)
                        sp.wait_ge(s_cd, b * 16 + 16)
                    sp.dma_start(weight[e], rows[e, :].partition_broadcast(128)).then_inc(s_cb[e], 16)

            spread(0)
            spread(1)
            with sp.Fori(1, LAST) as n:
                store(n - 1)
                spread(n + 1)
            store(LAST - 1)
            for h in range(2):
                sp.wait_ge(s_out, LAST + 1 + h)
                sp.dma_start(out_dram[LAST, :, some(h), :], result[:, some(h), :]).then_inc(s_store, 16)
            sp.wait_ge(s_store, 16 * (BATCHES + 1))

        @block.gpsimd
        def _(pool):
            g = nc.gpsimd
            made, taken = [0], [0]

            def link(ins):
                made[0] += 1
                ins.then_inc(s_pc, 1)
                pool.wait_ge(s_pc, made[0])

            def take_wait():
                taken[0] += 1
                k = taken[0] % SPARE
                g.tensor_tensor(spare_p[:, k:k + 1], neg_one[:, 0:1], neg_one[:, 0:1], ALU.mult)
            g.memset(half_pow[:, :], 0.5)
            g.memset(neg_half[:, :], -0.5)
            g.memset(ones[:, :].bitcast(f32), 1.0)
            g.memset(eps[:, :], EPS)
            g.memset(neg_one[:, :], -1.0)
            link(g.memset(ident[:, :], 0.0))
            g.affine_select(out=ident[:, :], in_=ident[:, :], compare_op=ALU.not_equal, fill=1.0, base=0,
                            pattern=[[-1, 128]], channel_multiplier=1).then_inc(s_ident, 1)
            pool.wait_ge(s_par, 16)
            link(g.tensor_tensor(ecs[:, 0:2], par[:, P_RE:P_RE + 2], par[:, P_RE:P_RE + 2], ALU.mult))
            link(g.tensor_tensor(ecs[:, 2:3], ecs[:, 0:1], ecs[:, 1:2], ALU.add))
            g.tensor_tensor(ecs[:, 3:4], ecs[:, 2:3], half_pow[:, 0:1], ALU.pow).then_inc(s_mag, 1)

            def decay():
                pool.wait_ge(s_mag, 1)
                y, q = ecs[:, 4:5], ecs[:, 5:6]
                link(g.tensor_scalar(y, ecs[:, 3:4], EXP_LARGEST, None, ALU.min))
                for k in range(EXP_DEGREE):
                    last = g.tensor_scalar(yk[:, k:k + 1], y, -1.0 / 2 ** EXP_HALVINGS, 1.0 / (k + 1), ALU.mult, ALU.mult)
                link(last)
                link(g.tensor_scalar(q, yk[:, EXP_DEGREE - 1:EXP_DEGREE], 1.0, None, ALU.add))
                for k in reversed(range(1, EXP_DEGREE - 1)):
                    link(g.tensor_scalar(q, q, yk[:, k:k + 1], 1.0, ALU.mult, ALU.add))
                link(g.tensor_tensor(q, q, yk[:, 0:1], ALU.mult))
                for _ in range(EXP_HALVINGS):
                    link(g.tensor_scalar(q, q, 2.0, q, ALU.add, ALU.mult))
                g.tensor_scalar(ecs[:, 6:7], q, 1.0, None, ALU.add).then_inc(s_decay, 1)

            def emit(i, base):
                ticks = 0
                b1, b2, b3 = i + 1, i + 2, i + 3

                def then(ins):
                    nonlocal ticks
                    ins.then_inc(s_po, 1)
                    ticks += 1
                    pool.wait_ge(s_po, base + ticks)
                if live(b3):
                    pool.wait_ge(s_x0m, b3 + 1)
                    after(pool, s_hn, b3)
                    var = mom0[:, :, 1]
                    g.tensor_tensor(var_eps[:, 0, :], var, eps[:, :], ALU.add)
                    g.tensor_tensor(tmp[:, 2, :], mom0[:, :, 0], neg_one[:, :], ALU.mult)
                    then(g.tensor_scalar(var_eps[:, 1, :], var, 1.0 + EPS, EPS * EPS, ALU.mult, ALU.add))
                    then(g.tensor_tensor(norm_pow[:, :, :].rearrange("p a b -> p (a b)"),
                                         var_eps[:, :, :].rearrange("p a b -> p (a b)"), neg_half[:, :], ALU.pow))
                    g.tensor_tensor(shift0[:, :], tmp[:, 2, :], norm_pow[:, 1, :], ALU.mult).then_inc(s_sc0, 1)
                if live(b1):
                    pool.wait_ge(s_x1m, b1 + 1)
                    after(pool, s_h2, b1)
                    g.tensor_tensor(tmp[:, 0, :], mom1[:, :, 0], neg_one[:, :], ALU.mult)
                    then(g.tensor_tensor(tmp[:, 1, :], mom1[:, :, 1], eps[:, :], ALU.add))
                    then(g.tensor_tensor(scale1[:, :], tmp[:, 1, :], neg_half[:, 0:TPB], ALU.pow))
                    g.tensor_tensor(shift1[:, :], tmp[:, 0, :], scale1[:, :], ALU.mult).then_inc(s_sc1, 1)
                if live(b2):
                    if isinstance(b2, int) and b2 == 0:
                        pool.wait_ge(s_tab, 1)
                    pool.wait_ge(s_u, b2 + 1)
                    after(pool, s_conv, b2)
                    g.tensor_tensor(vi, u, in_im, ALU.mult).then_inc(s_ui, 1)
                    pool.wait_ge(s_vi, b2 + 1)
                    g.tensor_tensor(vi, vi, out_im, ALU.mult).then_inc(s_ti, 1)
                if live(b1):
                    r = batch_of(resid, b1)
                    pool.wait_ge(s_x1, b1 + 1)
                    take_wait()
                    g.tensor_tensor(r, r, x1, ALU.add).then_inc(s_base, 1)
                if live(b3):
                    pool.wait_ge(s_sc0, b3 + 1)
                    after(pool, s_xn, b3)
                    then(g.tensor_tensor(tmp[:, 3, :], var_eps[:, 1, :], norm_pow[:, 1, :], ALU.mult))
                    g.tensor_tensor(unscale0[:, :, 0], tmp[:, 3, :], norm_pow[:, 0, :], ALU.mult).then_inc(s_un, 1)
                return ticks

            base = emit(-3, 0)
            decay()
            pool.wait_ge(s_low_high, 1)
            g.tensor_tensor(grid(out_im), slow[0], fast[1], ALU.mult)
            g.tensor_tensor(grid(in_im), slow[1], fast[0], ALU.mult).then_inc(s_oim, 1)
            for i in range(-2, 1):
                base += emit(i, base)
            whole = 2 + 2 + 1
            with pool.Fori(1, LAST - 3) as i:
                n = emit(i, (i - 1) * whole + base)
                assert n == whole
            base += whole * (LAST - 4)
            for i in range(LAST - 3, LAST):
                base += emit(i, base)

            def x2_scales(b, at):
                pool.wait_ge(s_x2m, b + 1)
                g.tensor_tensor(tmp[:, 6, :], mom2[:, :, 0], neg_one[:, :], ALU.mult)
                g.tensor_tensor(tmp[:, 7, :], mom2[:, :, 1], eps[:, :], ALU.add).then_inc(s_po, 1)
                pool.wait_ge(s_po, at + 1)
                g.tensor_tensor(scale2[:, :], tmp[:, 7, :], neg_half[:, 0:TPB], ALU.pow).then_inc(s_po, 1)
                pool.wait_ge(s_po, at + 2)
                g.tensor_tensor(shift2[:, :], tmp[:, 6, :], scale2[:, :], ALU.mult).then_inc(s_sc2, 1)

            def experts(n, q, more):
                for e in range(1, EXPERTS - 1 if isinstance(n, int) and n == LAST else EXPERTS):
                    pool.wait_ge(s_mul, n * (2 * EXPERTS) + (2 * e + 2))
                    after(pool, s_add, n * (EXPERTS - 1) + (e - 1))
                    g.tensor_tensor(total[q], total[q], part[e % 2], ALU.add).then_inc(s_add, 1)
                    if e == 3 and more:
                        x2_scales(n + 2, n * 2 + (base + 4))
            x2_scales(0, base)
            x2_scales(1, base + 2)
            experts(0, 0, True)
            with pool.Fori(0, (LAST - 3) // 2) as m:
                experts(m * 2 + 1, 1, True)
                experts(m * 2 + 2, 0, True)
            experts(LAST - 2, 1, True)
            experts(LAST - 1, 0, False)
            experts(LAST, 1, False)

        @block.scalar
        def _(a):
            s = nc.scalar
            a.wait_ge(s_par, 16)

            def emit(i, pieces=()):
                b1, b2, b3 = i + 1, i + 2, i + 3
                pieces = list(pieces)

                def piece():
                    if pieces:
                        pieces.pop(0)()

                def mlp_act(c):
                    a.wait_ge(s_up, i * FC + (c + 1))
                    after(a, s_dn, i * FC + (c - 1))
                    s.activation(silu[c % 2], up_p[c % 2][:, :], ACT.Silu, bias=b1_all[:, c:c + 1]).then_inc(s_silu, 1)
                if live(i):
                    mlp_act(0)
                    mlp_act(1)
                if live(b2):
                    a.wait_ge(s_t1, b2 + 1)
                    after(a, s_t2, b2)
                    s.activation(u, turn_p[:, :], ACT.Identity, bias=par[:, BETA:BETA + 1],
                                 scale=par[:, GAMMA:GAMMA + 1]).then_inc(s_u, 1)
                if live(b1):
                    a.wait_ge(s_sc1, b1 + 1)
                    after(a, s_t3, b1)
                    for j in range(TPB):
                        last = s.activation(h2[:, j, :], x1[:, j, :], ACT.Identity, bias=shift1[:, j:j + 1],
                                            scale=scale1[:, j:j + 1])
                    last.then_inc(s_h2, 1)
                piece()
                if live(i):
                    mlp_act(2)
                piece()
                if live(i):
                    mlp_act(3)
                if live(b1):
                    a.wait_ge(s_t3, b1 + 1)
                    s.activation(h_hi[:, :], turn_p[:, :], ACT.Copy).then_inc(s_hi, 1)
                if live(b3):
                    a.wait_ge(s_sc0, b3 + 1)
                    after(a, s_t1, b3)
                    after(a, s_xn, b3)
                    for j in range(TPB):
                        last = s.activation(hn[:, j, :], tile_of(resid, b3, j), ACT.Identity, bias=shift0[:, j:j + 1],
                                            scale=norm_pow[:, 1, j:j + 1])
                    last.then_inc(s_hn, 1)
                while pieces:
                    piece()

            def norm(b, part=None):
                if part in (None, 0):
                    a.wait_ge(s_sc2, b + 1)
                    after(a, s_t4, b)
                tiles = range(TPB) if part is None else range(part * TPB // 4, (part + 1) * TPB // 4)
                for j in tiles:
                    last = s.activation(xm[:, j, :], tile_of(resid, b, j), ACT.Identity, bias=shift2[:, j:j + 1],
                                        scale=scale2[:, j:j + 1])
                if part in (None, 3):
                    last.then_inc(s_xm, 1)

            def high(b, q):
                a.wait_ge(s_t4, b + 1)
                after(a, s_mup, b * (EC * EXPERTS) - EC * EXPERTS)
                s.activation(xm_hi[q][:, :], turn_p[:, :], ACT.Copy).then_inc(s_xhi, 1)

            def logits_copy(b):
                a.wait_ge(s_rt, b + 1)
                s.activation(logit_t, turn_p[0:EXPERTS, :], ACT.Copy).then_inc(s_lt, 1)

            def tanh(b):
                a.wait_ge(s_gap, b + 1)
                s.activation(th[:, :, :], gap[:, :, :], ACT.Tanh, scale=0.5).then_inc(s_tanh, 1)

            def comb_copy(b):
                a.wait_ge(s_cm, b + 1)
                after(a, s_cd, b * 16)
                s.activation(comb_t, turn_p[0:EXPERTS, :], ACT.Copy).then_inc(s_ct, 1)

            def expert_weights():
                a.wait_ge(s_mw, 16 * 2)
                s.activation(mw2_hi[:, :], mw2_sb, ACT.Copy)
                s.activation(mw1_hi[:, :], mw1_sb, ACT.Copy).then_inc(s_mwhi, 1)

            emit(-3)
            a.wait_ge(s_ore, 1)
            s.activation(in_re, out_re, ACT.Copy, scale=par[:, INIT_RE:INIT_RE + 1])
            s.activation(vi, out_re, ACT.Copy, scale=par[:, INIT_IM:INIT_IM + 1]).then_inc(s_ire, 1)
            for i in range(-2, 0):
                emit(i)
            a.wait_ge(s_b1, 1)
            emit(0)
            with a.Fori(1, LAST - 3) as i:
                emit(i)
            for i in range(LAST - 3, LAST - 2):
                emit(i)
            emit(LAST - 2)
            expert_weights()
            emit(LAST - 1)
            norm(0)
            emit(LAST, (lambda: high(0, 0), lambda: logits_copy(0), lambda: tanh(0)))

            def gelu(n, e, c):
                a.wait_ge(s_mup, n * (EC * EXPERTS) + (EC * e + c + 1))
                after(a, s_elo, n * (EC * EXPERTS) + (EC * (e - 2) + c + 1))
                k = MB1 + e * EC + c
                s.activation(hid[c][e % 2], up_p[c][:, :], ACT.Gelu, bias=par[:, k:k + 1]).then_inc(s_gelu, 1)

            def hid_high(n, e, c, done):
                a.wait_ge(s_gelu, n * (EC * EXPERTS) + (EC * e + c + 1))
                after(a, s_edn, n * (2 * EXPERTS) + 2 * (e - 1))
                s.activation(hid_hi[c][e % 2][:, :], hid[c][e % 2], ACT.Copy).then_inc(done, 1)

            def both(n, e, first=None, second=None):
                gelu(n, e, 0)
                hid_high(n, e, 0, s_hi0)
                if first is not None:
                    first()
                gelu(n, e, 1)
                if second is not None:
                    second()
                hid_high(n, e, 1, s_hi1)

            def experts(n, q, more, second):
                for e in range(EXPERTS):
                    if more:
                        if e == 2:
                            high(n + 1, 1 - q)
                        if e == 3:
                            logits_copy(n + 1)
                    if e + 1 < EXPERTS:
                        both(n, e + 1, (lambda: tanh(n + 1)) if more and e == 6 else None)
                    elif more:
                        both(n + 1, 0, None, lambda: comb_copy(n + 1))
                    if e == 0 and isinstance(n, int) and n == 0:
                        norm(1)
                    if second and e >= 4:
                        norm(n + 2, e - 4)
            both(0, 0, None, lambda: comb_copy(0))
            experts(0, 0, True, True)
            with a.Fori(0, (LAST - 3) // 2) as m:
                experts(m * 2 + 1, 1, True, True)
                experts(m * 2 + 2, 0, True, True)
            experts(LAST - 2, 1, True, True)
            experts(LAST - 1, 0, True, False)
            experts(LAST, 1, False, False)

        @block.tensor
        def _(pe):
            t = nc.tensor

            def turned(src, done):
                for j in range(TPB):
                    last = t.transpose(turn_p[:, j * TILE:(j + 1) * TILE], src(j), ident[:, :])
                last.then_inc(done, 1)

            def split_product(dst, terms, done=None):
                for k, (w_hi, w_lo, x_hi, x_lo) in enumerate(terms):
                    t.matmul(dst, w_hi, x_lo, start=k == 0, stop=False)
                    t.matmul(dst, w_hi, x_hi, start=False, stop=False)
                    last = t.matmul(dst, w_lo, x_hi, start=False, stop=k == len(terms) - 1)
                if done is not None:
                    last.then_inc(done, 1)

            def up(dst, hi, lo, w_hi, w_lo, done):
                for h in range(2):
                    split_product(half(dst, h), [(w_hi, w_lo, half(hi, h), half(lo, h))], done if h else None)

            def mlp_up(i, c):
                after(pe, s_silu, i * FC + (c - 1))
                k = slice(c * 128, (c + 1) * 128)
                up(up_p[c % 2], h_hi, h_lo, w1_hi[:, k], w1_lo[:, k], s_up)

            def mlp_down(i, c):
                if c == 0:
                    after(pe, s_x2, i)
                    for h in range(2):
                        t.matmul(half(down_p, h), ones[:, :], b2_hi_lo[:, :], start=True, stop=False, skip_group_check=True)
                pe.wait_ge(s_silu, i * FC + (c + 1))
                for j in range(TPB):
                    last = t.matmul(down_p[:, j * D:(j + 1) * D], silu[c % 2][:, j * TILE:(j + 1) * TILE], w2_sb[:, c, :],
                                    start=False, stop=c == FC - 1, skip_group_check=True)
                last.then_inc(s_dn, 1)

            def emit(i, pieces=()):
                b1, b2 = i + 1, i + 2
                pieces = list(pieces)

                def piece():
                    if pieces:
                        pieces.pop(0)()
                if live(b1):
                    pe.wait_ge(s_conv, b1 + 1)
                    after(pe, s_lo, b1)
                    turned(lambda j: u[:, j * TILE:(j + 1) * TILE], s_t2)
                if live(i):
                    pe.wait_ge(s_lo, i + 1)
                    mlp_up(i, 0)
                    mlp_up(i, 1)
                if live(b2):
                    pe.wait_ge(s_hn, b2 + 1)
                    after(pe, s_x1, b2)
                    turned(lambda j: hn[:, j, :], s_t1)
                piece()
                if live(i):
                    mlp_down(i, 0)
                    mlp_up(i, 2)
                    piece()
                    mlp_down(i, 1)
                    mlp_up(i, 3)
                    piece()
                if live(b1):
                    pe.wait_ge(s_h2, b1 + 1)
                    if live(b2):
                        pe.wait_ge(s_u, b2 + 1)
                    turned(lambda j: h2[:, j, :], s_t3)
                if live(i):
                    mlp_down(i, 2)
                    mlp_down(i, 3)

            def xm_turn(b):
                pe.wait_ge(s_xm, b + 1)
                after(pe, s_out, b - 1)
                if isinstance(b, int) and b == 0:
                    pe.wait_ge(s_lo, BATCHES)
                if isinstance(b, int) and b == 1:
                    pe.wait_ge(s_ct, 1)
                turned(lambda j: xm[:, j, :], s_t4)

            def route(b, q):
                pe.wait_ge(s_xlo, b + 1)
                up(turn_p, xm_hi[q], xm_lo[q], router_hi[:, :], router_lo[:, :], s_rt)

            def logits_turn(b):
                pe.wait_ge(s_lt, b + 1)
                for j in range(TPB):
                    dst, src = turn_p[:, j * EXPERTS:(j + 1) * EXPERTS], logit_t[:, j * TILE:(j + 1) * TILE]
                    if j == 0:
                        last = t.matmul(dst, src, ident[0:EXPERTS, 0:EXPERTS], start=True, stop=True)
                    else:
                        last = t.transpose(dst, src, ident[0:EXPERTS, 0:EXPERTS])
                last.then_inc(s_tn, 1)

            def comb_turn(b):
                pe.wait_ge(s_comb, b + 1)
                for j in range(TPB):
                    last = t.transpose(turn_p[0:EXPERTS, j * TILE:(j + 1) * TILE], comb[:, j, :], ident[:, :])
                last.then_inc(s_cm, 1)

            def total_turn(n, q):
                pe.wait_ge(s_add, n * (EXPERTS - 1) + (EXPERTS - 1))
                pe.wait_ge(s_ct, n + 2)
                turned(lambda j: total[q][:, j * TILE:(j + 1) * TILE], s_otr)

            pe.wait_ge(s_ident, 1)
            pe.wait_ge(s_w, 16 * 4)
            pe.wait_ge(s_par, 16)
            for c in range(FC):
                last = t.matmul(down_p[:, c:c + 1], w1_sb[:, c * 128:(c + 1) * 128], par[:, BETA:BETA + 1],
                                start=True, stop=True)
            last.then_inc(s_b1raw, 1)
            for i in range(-2, 0):
                emit(i)
            pe.wait_ge(s_wsplit, 1)
            pe.wait_ge(s_b1, 1)
            emit(0)
            with pe.Fori(1, LAST - 3) as i:
                emit(i)
            for i in range(LAST - 3, LAST):
                emit(i)
            emit(LAST, (lambda: xm_turn(0), lambda: route(0, 0), lambda: logits_turn(0)))

            def expert_up(n, e, q):
                if e == 0:
                    pe.wait_ge(s_xlo, n + 1)
                for c in range(EC):
                    if isinstance(n, int) and n == 0 and e == 0:
                        pe.wait_ge(s_silu, BATCHES * FC - EC + c + 1)
                    after(pe, s_gelu, n * (EC * EXPERTS) + (EC * (e - 1) + c + 1))
                    k = slice((e * EC + c) * 128, (e * EC + c + 1) * 128)
                    up(up_p[c], xm_hi[q], xm_lo[q], mw1_hi[:, k], mw1_lo[:, k], s_mup)

            def expert_down(n, e):
                if isinstance(n, int) and n == 0 and e == 0:
                    pe.wait_ge(s_x2, BATCHES)
                pe.wait_ge(s_elo, n * (EC * EXPERTS) + (EC * e + EC))
                for h in range(2):
                    after(pe, s_mul, n * (2 * EXPERTS) + (2 * (e - 1) + h + 1))
                    terms = []
                    for c in range(EC):
                        k = slice((e * EC + c) * D, (e * EC + c + 1) * D)
                        terms.append((mw2_hi[:, k], mw2_lo[:, k], half(hid_hi[c][e % 2], h), half(hid_lo[c][e % 2], h)))
                    split_product(half(down_p, h), terms, s_edn)

            def experts(n, q, before, more):
                for e in range(EXPERTS):
                    if e + 1 < EXPERTS:
                        expert_up(n, e + 1, q)
                    elif more:
                        expert_up(n + 1, 0, 1 - q)
                        comb_turn(n + 1)
                    expert_down(n, e)
                    if e == 0 and before:
                        total_turn(n - 1, 1 - q)
                    if more:
                        if e == 1:
                            xm_turn(n + 1)
                        if e == 2:
                            route(n + 1, 1 - q)
                        if e == 3:
                            logits_turn(n + 1)
            expert_up(0, 0, 0)
            comb_turn(0)
            experts(0, 0, False, True)
            with pe.Fori(0, (LAST - 3) // 2) as m:
                experts(m * 2 + 1, 1, True, True)
                experts(m * 2 + 2, 0, True, True)
            experts(LAST - 2, 1, True, True)
            experts(LAST - 1, 0, True, True)
            experts(LAST, 1, True, False)
            pe.wait_ge(s_out, LAST)
            for h in range(2):
                pe.wait_ge(s_last, h + 1)
                for j in range(TPB)[some(h)]:
                    last = t.transpose(turn_p[:, j * TILE:(j + 1) * TILE], total[1][:, j * TILE:(j + 1) * TILE],
                                       ident[:, :])
                last.then_inc(s_lotr, 1)

        @block.vector
        def _(v):
            d = nc.vector
            made, taken = [0], [0]

            def link(ins):
                made[0] += 1
                ins.then_inc(s_vc, 1)
                v.wait_ge(s_vc, made[0])

            def take_wait():
                taken[0] += 1
                k = taken[0] % SPARE
                d.memset(spare_v[:, k:k + 1], 0.0)

            def statistics(src, stats, tiles=range(TPB)):
                take_wait()
                for j in tiles:
                    last = d.bn_stats(stats[:, j, :], src(j))
                return last

            def aggregates(stats, mom, done):
                take_wait()
                for j in range(TPB):
                    last = d.bn_aggr(mom[:, j, :], stats[:, j, :])
                last.then_inc(done, 1)

            def moments(src, stats, mom, at, done):
                statistics(src, stats).then_inc(s_vo, 1)
                v.wait_ge(s_vo, at + 1)
                aggregates(stats, mom, done)

            def emit(i, base, piece=None):
                ticks = 0
                first = isinstance(i, int) and i == -2
                b0, b1, b2, b4 = i - 1, i + 1, i + 2, i + 4

                def then(ins):
                    nonlocal ticks
                    ins.then_inc(s_vo, 1)
                    ticks += 1
                    v.wait_ge(s_vo, base + ticks)
                if live(b0):
                    v.wait_ge(s_dn, i * FC)
                    v.wait_ge(s_base, i)
                    r = batch_of(resid, b0)
                    d.tensor_tensor(r, tiled(down_p[:, :]), r, ALU.add).then_inc(s_x2, 1)
                if live(b1):
                    v.wait_ge(s_t2, b1 + 1)
                    v.wait_ge(s_xn, b1 + 1)
                    after(v, s_base, b1)
                    after(v, s_h2, b1)
                    d.tensor_tensor(x1, xn, tiled(turn_p[:, :]), ALU.add).then_inc(s_x1, 1)
                    v.wait_ge(s_x1, b1 + 1)
                    after(v, s_sc1, b1)
                    moments(lambda j: x1[:, j, :], stats1, mom1, base + ticks, s_x1m)
                    ticks += 1

                def rotate():
                    decay = ecs[:, 6:7].to_broadcast([128, LENGTH])
                    v.wait_ge(s_u, b2 + 1)
                    then(d.tensor_tensor(vr, u, in_re, ALU.mult))
                    then(d.tensor_tensor_scan(vr, decay, vr, cst[:, 16:17], ALU.mult, ALU.add))
                    v.wait_ge(s_ui, b2 + 1)
                    d.tensor_tensor_scan(vi, decay, vi, cst[:, 17:18], ALU.mult, ALU.add).then_inc(s_vi, 1)
                    then(d.tensor_tensor(vr, vr, out_re, ALU.mult))

                def convolution():
                    v.wait_ge(s_ti, b2 + 1)
                    d.tensor_tensor(u, vr, vi, ALU.subtract).then_inc(s_conv, 1)
                if first:
                    rotate()
                if live(b2):
                    v.wait_ge(s_hn, b2 + 1)
                    v.wait_ge(s_un, b2 + 1)
                    d.tensor_tensor(xn, hn, unscale0[:, :, :].to_broadcast([128, TPB, D]), ALU.mult).then_inc(s_xn, 1)
                if first:
                    convolution()
                if live(b4):
                    v.wait_ge(s_x, b4 * 16 + 16)
                    after(v, s_sc0, b4)
                    moments(lambda j: tile_of(resid, b4, j), stats0, mom0, base + ticks, s_x0m)
                    ticks += 1
                if piece is not None:
                    piece()
                if live(b2) and not first:
                    rotate()
                if live(b1):
                    v.wait_ge(s_hi, b1 + 1)
                    d.tensor_tensor(h_lo[:, :], turn_p[:, :], h_hi[:, :].bitcast(f32), ALU.subtract).then_inc(s_lo, 1)
                if live(b2) and not first:
                    convolution()
                return ticks

            def weights():
                v.wait_ge(s_w, 16 * 4)
                v.wait_ge(s_ident, 1)
                link(d.tensor_copy(b2_hi, b2_rows))
                link(d.tensor_tensor(b2_lo, b2_rows, b2_hi.bitcast(f32), ALU.subtract))
                link(d.tensor_scalar(b2_rows, b2_hi.bitcast(f32), ident[0:2, 0:1], None, ALU.mult))
                d.scalar_tensor_tensor(out=b2_hi_lo[:, :], in0=b2_lo, scalar=ident[0:2, 1:2], in1=b2_rows,
                                       op0=ALU.mult, op1=ALU.add)
                link(d.tensor_scalar(w1_g, w1_sb, par[:, GAMMA:GAMMA + 1], None, ALU.mult))
                link(d.tensor_copy(w1_hi[:, :], w1_g))
                d.tensor_tensor(w1_lo[:, :], w1_g, w1_hi[:, :].bitcast(f32), ALU.subtract).then_inc(s_wsplit, 1)
                v.wait_ge(s_b1raw, 1)
                d.tensor_tensor(b1_all[:, :], down_p[:, 0:FC], par[:, B1:B1 + FC], ALU.add).then_inc(s_b1, 1)

            def expert_weights():
                v.wait_ge(s_mw, 16 * 2)
                d.memset(router_hi[:, :].bitcast(f32), 0.0)
                link(d.memset(router_lo[:, :].bitcast(f32), 0.0))
                link(d.tensor_copy(router_hi[:, 0:EXPERTS], router_sb[:, :]))
                v.wait_ge(s_mwhi, 1)
                d.tensor_tensor(router_lo[:, 0:EXPERTS], router_sb[:, :], router_hi[:, 0:EXPERTS].bitcast(f32),
                                ALU.subtract)
                d.tensor_tensor(mw2_lo[:, :], mw2_sb, mw2_hi[:, :].bitcast(f32), ALU.subtract)
                d.tensor_tensor(mw1_lo[:, :], mw1_sb, mw1_hi[:, :].bitcast(f32), ALU.subtract).then_inc(s_wsplit, 1)
                for e in range(EXPERTS):
                    last = d.memset(rank[:, :, e:e + 1], float(EXPERTS - e))
                link(last)

            def tables(between):
                v.wait_ge(s_mag, 1)
                link(d.reciprocal(cst[:, 0:1], ecs[:, 3:4]))
                link(d.tensor_scalar(zz[:, 0, :], par[:, P_RE:P_RE + 2], cst[:, 0:1], None, ALU.mult))
                for k in range(1, POWERS):
                    d.tensor_tensor(sq[:, 0:2], zz[:, k - 1, :], zz[:, k - 1, :], ALU.mult)
                    link(d.tensor_tensor(sq[:, 2:3], zz[:, k - 1, 0:1], zz[:, k - 1, 1:2], ALU.mult))
                    d.tensor_tensor(zz[:, k, 0:1], sq[:, 0:1], sq[:, 1:2], ALU.subtract)
                    link(d.tensor_scalar(zz[:, k, 1:2], sq[:, 2:3], 2.0, None, ALU.mult))
                    if k % 2 == 0 or k == POWERS - 1:
                        link(d.tensor_tensor(sq[:, 0:2], zz[:, k, :], zz[:, k, :], ALU.mult))
                        link(d.tensor_tensor(sq[:, 3:4], sq[:, 0:1], sq[:, 1:2], ALU.add))
                        link(d.tensor_scalar(sq[:, 3:4], sq[:, 3:4], -0.5, 1.5, ALU.mult, ALU.add))
                        link(d.tensor_scalar(zz[:, k, :], zz[:, k, :], sq[:, 3:4], None, ALU.mult))
                link(d.tensor_scalar(cst[:, 16:18], par[:, LAST_RE:LAST_RE + 2], zz[:, 0, 0:1], None, ALU.mult))
                link(d.tensor_scalar(cst[:, 18:20], par[:, LAST_RE:LAST_RE + 2], zz[:, 0, 1:2], None, ALU.mult))
                d.tensor_tensor(cst[:, 16:17], cst[:, 16:17], cst[:, 19:20], ALU.subtract)
                d.tensor_tensor(cst[:, 17:18], cst[:, 17:18], cst[:, 18:19], ALU.add)
                re, im = low_high[:, 0, :, :], low_high[:, 1, :, :]
                d.memset(re[:, :, 0:1], 1.0)
                link(d.memset(im[:, :, 0:1], 0.0))
                d.tensor_scalar(cst[:, 20:21], par[:, INIT_RE:INIT_RE + 1], -1.0, None, ALU.mult)
                n, k = 1, 0
                while n < STEP:
                    z_re = zz[:, k::POWERS // 2, 0:1].to_broadcast([128, 2, n])
                    z_im = zz[:, k::POWERS // 2, 1:2].to_broadcast([128, 2, n])
                    p = [prod[:, m, :, 0:n] for m in range(4)]
                    d.tensor_tensor(p[0], re[:, :, 0:n], z_re, ALU.mult)
                    d.tensor_tensor(p[1], im[:, :, 0:n], z_im, ALU.mult)
                    d.tensor_tensor(p[2], re[:, :, 0:n], z_im, ALU.mult)
                    link(d.tensor_tensor(p[3], im[:, :, 0:n], z_re, ALU.mult))
                    d.tensor_tensor(re[:, :, n:2 * n], p[0], p[1], ALU.subtract)
                    last = d.tensor_tensor(im[:, :, n:2 * n], p[2], p[3], ALU.add)
                    n, k = 2 * n, k + 1
                    if n < STEP:
                        link(last)
                last.then_inc(s_low_high, 1)
                v.wait_ge(s_low_high, 1)
                d.tensor_tensor(grid(out_re), slow[0], fast[0], ALU.mult)
                link(d.tensor_tensor(grid(vr), slow[1], fast[1], ALU.mult))
                d.tensor_tensor(out_re, out_re, vr, ALU.subtract).then_inc(s_ore, 1)
                between()
                v.wait_ge(s_oim, 1)
                link(d.tensor_tensor(out_im, out_im, in_im, ALU.add))
                v.wait_ge(s_ire, 1)
                d.scalar_tensor_tensor(out=in_im, in0=out_im, scalar=cst[:, 20:21], in1=vi, op0=ALU.mult, op1=ALU.add)
                d.scalar_tensor_tensor(out=in_re, in0=out_im, scalar=par[:, INIT_IM:INIT_IM + 1], in1=in_re,
                                       op0=ALU.mult, op1=ALU.add).then_inc(s_tab, 1)

            SOME = 5

            def x2_stats(b, part=None, at=None):
                src = lambda j: tile_of(resid, b, j)
                if part != 1:
                    v.wait_ge(s_x2, b + 1)
                    after(v, s_sc2, b)
                    last = statistics(src, stats2, range(TPB if part is None else SOME))
                if part == 1:
                    last = statistics(src, stats2, range(SOME, TPB))
                if part != 0:
                    last.then_inc(s_vo, 1)
                    v.wait_ge(s_vo, b + ((base if at is None else at) + 1))
                    aggregates(stats2, mom2, s_x2m)

            emit(-4, 0)
            v.wait_ge(s_par, 16)
            base = 1
            tables(lambda: emit(-3, base))
            base += 1
            v.wait_ge(s_decay, 1)
            v.wait_ge(s_tab, 1)
            base += emit(-2, base)
            weights()
            base += emit(-1, base)
            base += emit(0, base)
            whole = 1 + 1 + 3
            with v.Fori(1, LAST - 3) as i:
                n = emit(i, (i - 1) * whole + base)
                assert n == whole, n
            base += whole * (LAST - 4)
            for i in range(LAST - 3, LAST - 1):
                base += emit(i, base)

            def start_of_e():
                x2_stats(0, None, base + 1)
                expert_weights()
            base += emit(LAST - 1, base, start_of_e)

            def low(b, q):
                v.wait_ge(s_xhi, b + 1)
                d.tensor_tensor(xm_lo[q][:, :], turn_p[:, :], xm_hi[q][:, :].bitcast(f32), ALU.subtract)\
                    .then_inc(s_xlo, 1)

            def wide(ap):
                return ap.to_broadcast([128, TPB, EXPERTS])
            ORDER = 5 + 1 + 5 + 3

            class Choice:
                def __init__(self, b):
                    self.b, self.ticks = b, 0

                def then(self, ins):
                    ins.then_inc(s_tv, 1)
                    self.ticks += 1
                    v.wait_ge(s_tv, self.b * ORDER + self.ticks)

                def choose(self, top, onehot):
                    then = self.then
                    then(d.tensor_reduce(top[:, :, :], logits[:, :, :], AX, ALU.max))
                    then(d.tensor_tensor(scored[:, :, :], logits[:, :, :], wide(top[:, :, :]), ALU.is_equal))
                    then(d.tensor_tensor(scored[:, :, :], scored[:, :, :], wide(rank[:, :, :]), ALU.mult))
                    then(d.tensor_reduce(pick[:, :, :], scored[:, :, :], AX, ALU.max))
                    then(d.tensor_tensor(onehot[:, :, :], scored[:, :, :], wide(pick[:, :, :]), ALU.is_equal))

                def choose_first(self):
                    v.wait_ge(s_tn, self.b + 1)
                    d.tensor_copy(logits[:, :, :], turn_p[:, 0:TPB * EXPERTS].rearrange("p (t e) -> p t e", e=EXPERTS))\
                        .then_inc(s_lg, 1)
                    v.wait_ge(s_lg, self.b + 1)
                    self.choose(best, first)
                    self.then(d.scalar_tensor_tensor(out=logits[:, :, :], in0=first[:, :, :], scalar=-LARGE,
                                                     in1=logits[:, :, :], op0=ALU.mult, op1=ALU.add))

                def choose_second(self):
                    self.choose(runner, second)
                    d.tensor_tensor(gap[:, :, :], best[:, :, :], runner[:, :, :], ALU.subtract).then_inc(s_gap, 1)

                def probabilities(self):
                    v.wait_ge(s_tanh, self.b + 1)
                    after(v, s_cm, self.b)
                    d.tensor_scalar(prob[:, 0, :, :], th[:, :, :], 0.5, 0.5, ALU.mult, ALU.add)
                    self.then(d.tensor_scalar(prob[:, 1, :, :], th[:, :, :], -0.5, 0.5, ALU.mult, ALU.add))
                    self.then(d.tensor_tensor(first[:, :, :], first[:, :, :], wide(prob[:, 0, :, :]), ALU.mult))
                    self.then(d.tensor_tensor(second[:, :, :], second[:, :, :], wide(prob[:, 1, :, :]), ALU.mult))
                    d.tensor_tensor(comb[:, :, :], first[:, :, :], second[:, :, :], ALU.add).then_inc(s_comb, 1)
                    assert self.ticks == ORDER, self.ticks

            emit(LAST, base)
            low(0, 0)
            c = Choice(0)
            c.choose_first()
            c.choose_second()
            c.probabilities()
            emit(LAST + 1, base)
            x2_stats(1)

            def split(n, e):
                for c, high_done in ((0, s_hi0), (1, s_hi1)):
                    v.wait_ge(high_done, n * EXPERTS + (e + 1))
                    d.tensor_tensor(hid_lo[c][e % 2][:, :], hid[c][e % 2], hid_hi[c][e % 2][:, :].bitcast(f32),
                                    ALU.subtract).then_inc(s_elo, 1)
                    yield

            def scaled(n, q, e, h):
                if h == 0:
                    v.wait_ge(s_cb[e], n * 16 + 16)
                    if e > 0:
                        after(v, s_add, n * (EXPERTS - 1) + max(e - 2, 0))
                v.wait_ge(s_edn, n * (2 * EXPERTS) + (2 * e + h + 1))
                d.scalar_tensor_tensor(out=half(part[e % 2] if e else total[q], h), in0=half(down_p, h),
                                       scalar=par[:, MB2 + e:MB2 + e + 1], in1=half(weight[e], h),
                                       op0=ALU.add, op1=ALU.mult).then_inc(s_mul, 1)

            def finish(n):
                v.wait_ge(s_otr, n + 1)
                d.tensor_tensor(result, tiled(turn_p[:, :]), batch_of(resid, n), ALU.add).then_inc(s_out, 1)

            def experts(n, q, before, more, second):
                if more:
                    c = Choice(n + 1)
                for e in range(EXPERTS):
                    if more and e == 2:
                        low(n + 1, 1 - q)
                    halves = iter(())
                    if e + 1 < EXPERTS:
                        halves = split(n, e + 1)
                    elif more:
                        halves = split(n + 1, 0)
                    for h in range(2):
                        next(halves, None)
                        scaled(n, q, e, h)
                        if more and e == 6 and h == 0:
                            c.probabilities()
                        if not more and e == EXPERTS - 1:
                            if h == 0:
                                v.wait_ge(s_add, BATCHES * (EXPERTS - 1) - 1)
                            v.wait_ge(s_mul, BATCHES * 2 * EXPERTS - 1 + h)
                            d.tensor_tensor(half(total[q], h), half(total[q], h), half(part[e % 2], h), ALU.add)\
                                .then_inc(s_last, 1)
                    if e == 0 and before:
                        finish(n - 1)
                    if more:
                        if e == 4:
                            c.choose_first()
                        if e == 5:
                            c.choose_second()
                    if second and e in (1, 3):
                        x2_stats(n + 2, (e - 1) // 2)
            for _ in split(0, 0):
                pass
            experts(0, 0, False, True, True)
            with v.Fori(0, (LAST - 3) // 2) as m:
                experts(m * 2 + 1, 1, True, True, True)
                experts(m * 2 + 2, 0, True, True, True)
            experts(LAST - 2, 1, True, True, True)
            experts(LAST - 1, 0, True, True, False)
            experts(LAST, 1, True, False, False)
            v.wait_ge(s_store, LAST * 16)
            for h in range(2):
                v.wait_ge(s_lotr, h + 1)
                d.tensor_tensor(result[:, some(h), :], tiled(turn_p[:, :])[:, some(h), :],
                                batch_of(resid, LAST)[:, some(h), :], ALU.add).then_inc(s_out, 1)


def kernel(**inputs):
    import numpy as np
    import concourse.bacc as bacc
    from concourse.bass_utils import run_bass_kernel_spmd

    p = {k: np.asarray(v) for k, v in inputs.items()}
    a, f = "L0_attn_", "L0_ffn_"
    columns = [p[a + k][:, None] for k in ("ln_gamma", "ln_beta", "phazor_re", "phazor_im", "phazor_init_re",
                                           "phazor_init_im", "last_conv_re", "last_conv_im")]
    columns.append(p[a + "b1"].reshape(FC, 128).T)
    columns.append(p[f + "b1"].reshape(EXPERTS * EC, 128).T)
    columns.append(p[f + "b2"].T)
    arrays = {
        "x": p[a + "x"],
        "cols": np.concatenate(columns, axis=1),
        "w1": p[a + "w1"],
        "w2": p[a + "w2"],
        "b2": np.tile(p[a + "b2"], (2, HALF // D)),
        "router": p[f + "router_w"].T,
        "mw1": p[f + "w1"].reshape(EXPERTS * EF, D).T,
        "mw2": p[f + "w2"].transpose(0, 2, 1),
    }
    arrays = {f"in_{k}": np.ascontiguousarray(v) for k, v in arrays.items()}
    nc = bacc.Bacc("TRN2", target_bir_lowering=False, num_devices=1)
    args = [nc.dram_tensor(k, v.shape, mybir.dt.from_np(v.dtype), kind="ExternalInput").ap()
            for k, v in arrays.items()]
    args.append(nc.dram_tensor("out", (BATCHES, LENGTH, D), mybir.dt.float32, kind="ExternalOutput").ap())
    block_moe_kernel(nc, *args)
    return run_bass_kernel_spmd(nc, [arrays], core_ids=[0]).results[0]["out"]
```

```python
import concourse.bass as bass
from concourse import mybir
from contextlib import ExitStack

BATCHES, LENGTH, D = 8, 1024, 128
FF = 512
EXPERTS, EF = 8, 256
TILE = 128
TPB = LENGTH // TILE
TILES = BATCHES * TPB
HALF = 512
FC = FF // 128
EC = EF // 128
EPS = 1e-5
(GAMMA, BETA, P_RE, P_IM, INIT_RE, INIT_IM, LAST_RE, LAST_IM) = range(8)
B1 = 8
MB1 = B1 + FC
MB2 = MB1 + EXPERTS * EC
COLS = MB2 + EXPERTS
EXP_HALVINGS = 7
EXP_DEGREE = 10
EXP_LARGEST = 104.0
LARGE = 3.0e38
STEP = 32
POWERS = 10
SPARE = 8


def block_moe_kernel(nc, x, cols, w1, w2, b2, router, mw1, mw2, out):
    f32 = mybir.dt.float32
    f32r = mybir.dt.float32r
    ALU = mybir.AluOpType
    ACT = mybir.ActivationFunctionType
    AX = mybir.AxisListType.X

    x_dram = x.rearrange("b (j p) d -> b p j d", p=TILE)
    out_dram = out.rearrange("b (j p) d -> b p j d", p=TILE)

    ctx = ExitStack()
    with ctx:
        def sb(name, shape, dt=f32):
            return ctx.enter_context(nc.sbuf_tensor(name, shape, dt))

        def sem(name):
            return ctx.enter_context(nc.semaphore(name))

        resid = sb("resid", [128, TILES, D])
        par = sb("par", [128, COLS])
        w1_hi = sb("w1_hi", [128, FF], f32r)
        w1_lo = sb("w1_lo", [128, FF], f32r)
        w2_sb = sb("w2_sb", [128, FC, D])
        b1_all = sb("b1_all", [128, FC])
        b2_hi_lo = sb("b2_hi_lo", [2, HALF], f32r)
        ones = sb("ones", [2, 128], f32r)
        mw1_hi = sb("mw1_hi", [128, EXPERTS * EF], f32r)
        mw1_lo = sb("mw1_lo", [128, EXPERTS * EF], f32r)
        mw2_hi = sb("mw2_hi", [128, EXPERTS * EC * D], f32r)
        mw2_lo = sb("mw2_lo", [128, EXPERTS * EC * D], f32r)
        router_sb = sb("router_sb", [128, EXPERTS])
        router_hi = sb("router_hi", [128, 128], f32r)
        router_lo = sb("router_lo", [128, 128], f32r)
        ident = sb("ident", [128, 128])
        rank = sb("rank", [128, 1, EXPERTS])
        hid_hi = [[sb(f"hid_hi{c}{q}", [128, LENGTH], f32r) for q in range(2)] for c in range(EC)]
        hid_lo = [[sb(f"hid_lo{c}{q}", [128, LENGTH], f32r) for q in range(2)] for c in range(EC)]
        h_hi, h_lo = hid_hi[0][0], hid_lo[0][0]
        xm_hi = [sb(f"xm_hi{q}", [128, LENGTH], f32r) for q in range(2)]
        xm_lo = [sb(f"xm_lo{q}", [128, LENGTH], f32r) for q in range(2)]
        work = sb("work", [128, 20, LENGTH])

        def slot(k):
            return work[:, k, :]

        def tiled(ap):
            return ap.rearrange("p (j d) -> p j d", d=D)
        in_re, in_im, out_re, out_im = slot(0), slot(1), slot(2), slot(3)
        hn, xn = tiled(slot(4)), tiled(slot(5))
        u, vr, vi = slot(6), slot(7), slot(8)
        x1, h2 = tiled(slot(9)), tiled(slot(10))
        silu = [slot(11), slot(12)]
        mw1_sb = work[:, 13:15, :].rearrange("p a b -> p (a b)")
        mw2_sb = work[:, 15:17, :].rearrange("p a b -> p (a b)")
        b2_rows, b2_lo = work[0:2, 18, 0:HALF], work[0:2, 18, HALF:LENGTH]
        b2_hi = xm_hi[0][0:2, 0:HALF]
        b2_first = work[0:2, 19, 0:HALF]
        w1_sb, w1_g = work[:, 17, 0:FF], work[:, 17, FF:2 * FF]
        weight = [slot(e) for e in range(EXPERTS)]
        xm = tiled(slot(8))
        total = [slot(9), slot(10)]
        part = [slot(11), slot(12)]
        hid = [[slot(13), slot(14)], [slot(15), slot(16)]]
        result = tiled(slot(17))
        logit_t = work[0:EXPERTS, 18, :]
        comb_t = work[0:EXPERTS, 19, :]
        mag = sb("mag", [128, 7])
        abs_p, decay_factor = mag[:, 3:4], mag[:, 6:7]
        inv_abs = sb("inv_abs", [128, 1])
        start_v = sb("start_v", [128, 4])
        neg_init_re = sb("neg_init_re", [128, 1])
        yk = sb("yk", [128, EXP_DEGREE])
        zz = sb("zz", [128, POWERS, 2])
        sq = sb("sq", [128, 4])
        low_high = sb("low_high", [128, 2, 2, STEP])
        prod = sb("prod", [128, 4, 2, STEP])
        stats0 = sb("stats0", [128, TPB, 6])
        stats1 = sb("stats1", [128, TPB, 6])
        stats2 = sb("stats2", [128, TPB, 6])
        mom0 = sb("mom0", [128, TPB, 2])
        mom1 = sb("mom1", [128, TPB, 2])
        mom2 = sb("mom2", [128, TPB, 2])
        half_pow = sb("half_pow", [128, TPB])
        neg_half = sb("neg_half", [128, 2 * TPB])
        neg_one = sb("neg_one", [128, TPB])
        eps = sb("eps", [128, TPB])
        tmp = sb("tmp", [128, 8, TPB])
        var_eps = sb("var_eps", [128, 2, TPB])
        norm_pow = sb("norm_pow", [128, 2, TPB])
        shift0 = sb("shift0", [128, TPB])
        unscale0 = sb("unscale0", [128, TPB, 1])
        scale1 = sb("scale1", [128, TPB])
        shift1 = sb("shift1", [128, TPB])
        scale2 = sb("scale2", [128, TPB])
        shift2 = sb("shift2", [128, TPB])
        spare_v = sb("spare_v", [128, SPARE])
        spare_p = sb("spare_p", [128, SPARE])
        spare_a = sb("spare_a", [128, 2])
        logits = sb("logits", [128, TPB, EXPERTS])
        first = sb("first", [128, TPB, EXPERTS])
        second = sb("second", [128, TPB, EXPERTS])
        scored = sb("scored", [128, TPB, EXPERTS])
        comb = sb("comb", [128, TPB, EXPERTS])
        best = sb("best", [128, TPB, 1])
        runner = sb("runner", [128, TPB, 1])
        pick = sb("pick", [128, TPB, 1])
        gap = sb("gap", [128, TPB, 1])
        th = sb("th", [128, TPB, 1])
        prob = sb("prob", [128, 2, TPB, 1])
        comb_dram = nc.dram_tensor("comb_weights", (BATCHES, EXPERTS, LENGTH), f32, kind="Internal").ap()

        def pair(name):
            return ctx.enter_context(nc.psum_tensor(name, [128, LENGTH], f32))
        turn_p = pair("turn_p")
        up_p = [pair("up_p0"), pair("up_p1")]
        down_p = pair("down_p")

        s_par = sem("params_loaded")
        s_w = sem("weights_loaded")
        s_mw = sem("expert_weights_loaded")
        s_x = sem("x_loaded")
        s_cd = sem("comb_weights_stored")
        s_cb = [sem(f"comb_weights_spread{e}") for e in range(EXPERTS)]
        s_store = sem("block_stored")
        s_pc = sem("pool_const_order")
        s_vc = sem("vector_const_order")
        s_ident = sem("identity_ready")
        s_mag = sem("magnitude_ready")
        s_decay = sem("decay_ready")
        s_low_high = sem("table_factors_ready")
        s_ore = sem("out_re_ready")
        s_oim = sem("out_im_products_ready")
        s_ire = sem("init_products_ready")
        s_tab = sem("tables_ready")
        s_wsplit = sem("weights_split")
        s_aw = sem("scalar_weight_order")
        s_whi = sem("weights_high")
        s_mwhi = sem("expert_weights_high")
        s_b1raw = sem("bias_product_done")
        s_b1 = sem("bias_ready")
        s_po = sem("pool_order")
        s_vo = sem("vector_order")
        s_x0m = sem("x0_moments")
        s_sc0 = sem("x0_scales")
        s_un = sem("x0_unscale")
        s_hn = sem("hn_ready")
        s_xn = sem("xn_ready")
        s_t1 = sem("hn_turned")
        s_u = sem("u_ready")
        s_ui = sem("u_im_ready")
        s_vi = sem("v_im_ready")
        s_ti = sem("out_im_ready")
        s_conv = sem("conv_ready")
        s_t2 = sem("conv_turned")
        s_x1 = sem("x1_ready")
        s_x1m = sem("x1_moments")
        s_sc1 = sem("x1_scales")
        s_h2 = sem("h2_ready")
        s_base = sem("residual_ready")
        s_t3 = sem("h2_turned")
        s_hi = sem("h_hi_ready")
        s_lo = sem("h_lo_ready")
        s_up = sem("up_done")
        s_silu = sem("silu_done")
        s_dn = sem("down_done")
        s_x2 = sem("x2_ready")
        s_x2m = sem("x2_moments")
        s_sc2 = sem("x2_scales")
        s_xm = sem("xm_ready")
        s_t4 = sem("xm_turned")
        s_xhi = sem("xm_hi_ready")
        s_xlo = sem("xm_lo_ready")
        s_rt = sem("router_done")
        s_lt = sem("logits_t_ready")
        s_tn = sem("logits_turned")
        s_lg = sem("logits_ready")
        s_gap = sem("gap_ready")
        s_tanh = sem("tanh_ready")
        s_comb = sem("comb_ready")
        s_cm = sem("comb_turned")
        s_ct = sem("comb_t_ready")
        s_otr = sem("total_turned")
        s_out = sem("result_ready")
        s_last = sem("last_total_ready")
        s_lotr = sem("last_total_turned")
        s_tv = sem("choice_order")
        s_mup = sem("expert_up_done")
        s_gelu = sem("gelu_done")
        s_hi0 = sem("hid_hi0_ready")
        s_hi1 = sem("hid_hi1_ready")
        s_elo = sem("hid_lo_ready")
        s_edn = sem("expert_down_done")
        s_mul = sem("part_ready")
        s_add = sem("part_added")

        block = ctx.enter_context(nc.Block())
        LAST = BATCHES - 1

        def after(eng, semaphore, count):
            if not isinstance(count, int) or count > 0:
                eng.wait_ge(semaphore, count)

        def batch_of(t, b):
            return t[:, bass.ds(b * TPB, TPB), :]

        def tile_of(t, b, j):
            return t[:, bass.ds(b * TPB + j, 1), :].rearrange("p a d -> p (a d)")

        def half(ap, h):
            return ap[:, h * HALF:(h + 1) * HALF]

        fast = [low_high[:, m, 0:1, :].to_broadcast([128, STEP, STEP]) for m in range(2)]
        slow = [low_high[:, m, 1, :].unsqueeze(2).to_broadcast([128, STEP, STEP]) for m in range(2)]

        def grid(ap):
            return ap.rearrange("p (h l) -> p h l", l=STEP)

        def some(h):
            return slice(h * TPB // 2, (h + 1) * TPB // 2)

        class Step:
            turn = 0
            split = 1
            logits = 2
            first = 3
            second = 4
            probabilities = 5
            weights = 6
            total = 4
            finish = 5

        def live(b):
            return not isinstance(b, int) or 0 <= b <= LAST

        @block.sync
        def _(sp):
            sp.dma_start(par[:, :], cols).then_inc(s_par, 16)
            sp.dma_start(batch_of(resid, 0), x_dram[0, :, :, :]).then_inc(s_x, 16)
            for dst, src in ((w1_sb, w1), (w2_sb[:, :, :], w2.rearrange("(c p) d -> p c d", p=128)),
                             (b2_rows, b2), (router_sb[:, :], router)):
                sp.dma_start(dst, src).then_inc(s_w, 16)
            sp.dma_start(mw1_sb, mw1).then_inc(s_mw, 16)
            sp.dma_start(tiled(mw2_sb), mw2.rearrange("e (c p) d -> p (e c) d", p=128)).then_inc(s_mw, 16)
            with sp.Fori(1, BATCHES) as b:
                sp.wait_ge(s_x, b * 16)
                sp.dma_start(batch_of(resid, b), x_dram[bass.ds(b, 1), :, :, :].rearrange("a p j d -> (a p) j d"))\
                    .then_inc(s_x, 16)

            def store(n):
                sp.wait_ge(s_out, n + 1)
                sp.dma_start(out_dram[bass.ds(n, 1), :, :, :].rearrange("a p j d -> (a p) j d"), result)\
                    .then_inc(s_store, 16)

            def spread(b):
                sp.wait_ge(s_ct, b + 1)
                rows = comb_dram[bass.ds(b, 1), :, :].rearrange("a e t -> (a e) t")
                sp.dma_start(rows, comb_t).then_inc(s_cd, 16)
                for e in range(EXPERTS):
                    after(sp, s_mul, (b - 1) * (2 * EXPERTS) + (2 * e + 2))
                    if e == 0:
                        after(sp, s_store, (b - 1) * 16)
                        sp.wait_ge(s_cd, b * 16 + 16)
                    sp.dma_start(weight[e], rows[e, :].partition_broadcast(128)).then_inc(s_cb[e], 16)

            spread(0)
            spread(1)
            with sp.Fori(1, LAST) as n:
                store(n - 1)
                spread(n + 1)
            store(LAST - 1)
            for h in range(2):
                sp.wait_ge(s_out, LAST + 1 + h)
                sp.dma_start(out_dram[LAST, :, some(h), :], result[:, some(h), :]).then_inc(s_store, 16)
            sp.wait_ge(s_store, 16 * (BATCHES + 1))

        @block.gpsimd
        def _(pool):
            g = nc.gpsimd
            made, taken = [0], [0]

            def link(ins):
                made[0] += 1
                ins.then_inc(s_pc, 1)
                pool.wait_ge(s_pc, made[0])

            def take_wait():
                taken[0] += 1
                k = taken[0] % SPARE
                g.tensor_tensor(spare_p[:, k:k + 1], neg_one[:, 0:1], neg_one[:, 0:1], ALU.mult)
            g.memset(half_pow[:, :], 0.5)
            g.memset(neg_half[:, :], -0.5)
            g.memset(ones[:, :].bitcast(f32), 1.0)
            g.memset(eps[:, :], EPS)
            g.memset(neg_one[:, :], -1.0)
            link(g.memset(ident[:, :], 0.0))
            g.affine_select(out=ident[:, :], in_=ident[:, :], compare_op=ALU.not_equal, fill=1.0, base=0,
                            pattern=[[-1, 128]], channel_multiplier=1).then_inc(s_ident, 1)
            pool.wait_ge(s_par, 16)
            link(g.tensor_tensor(mag[:, 0:2], par[:, P_RE:P_RE + 2], par[:, P_RE:P_RE + 2], ALU.mult))
            link(g.tensor_tensor(mag[:, 2:3], mag[:, 0:1], mag[:, 1:2], ALU.add))
            g.tensor_tensor(abs_p, mag[:, 2:3], half_pow[:, 0:1], ALU.pow).then_inc(s_mag, 1)

            def decay():
                pool.wait_ge(s_mag, 1)
                y, q = mag[:, 4:5], mag[:, 5:6]
                link(g.tensor_scalar(y, abs_p, EXP_LARGEST, None, ALU.min))
                for k in range(EXP_DEGREE):
                    last = g.tensor_scalar(yk[:, k:k + 1], y, -1.0 / 2 ** EXP_HALVINGS, 1.0 / (k + 1),
                                           ALU.mult, ALU.mult)
                link(last)
                link(g.tensor_scalar(q, yk[:, EXP_DEGREE - 1:EXP_DEGREE], 1.0, None, ALU.add))
                for k in reversed(range(1, EXP_DEGREE - 1)):
                    link(g.tensor_scalar(q, q, yk[:, k:k + 1], 1.0, ALU.mult, ALU.add))
                link(g.tensor_tensor(q, q, yk[:, 0:1], ALU.mult))
                for _ in range(EXP_HALVINGS):
                    link(g.tensor_scalar(q, q, 2.0, q, ALU.add, ALU.mult))
                g.tensor_scalar(decay_factor, q, 1.0, None, ALU.add).then_inc(s_decay, 1)

            def iteration(i, base):
                ticks = 0
                b1, b2, b3 = i + 1, i + 2, i + 3

                def then(ins):
                    nonlocal ticks
                    ins.then_inc(s_po, 1)
                    ticks += 1
                    pool.wait_ge(s_po, base + ticks)

                def scales():
                    pool.wait_ge(s_x0m, b3 + 1)
                    after(pool, s_hn, b3)
                    var = mom0[:, :, 1]
                    g.tensor_tensor(var_eps[:, 0, :], var, eps[:, :], ALU.add)
                    g.tensor_tensor(tmp[:, 2, :], mom0[:, :, 0], neg_one[:, :], ALU.mult)
                    then(g.tensor_scalar(var_eps[:, 1, :], var, 1.0 + EPS, EPS * EPS, ALU.mult, ALU.add))
                    then(g.tensor_tensor(norm_pow[:, :, :].rearrange("p a b -> p (a b)"),
                                         var_eps[:, :, :].rearrange("p a b -> p (a b)"), neg_half[:, :], ALU.pow))
                    g.tensor_tensor(shift0[:, :], tmp[:, 2, :], norm_pow[:, 1, :], ALU.mult).then_inc(s_sc0, 1)
                late = isinstance(i, int) and i == -1
                if live(b3) and not late:
                    scales()
                if live(b1):
                    pool.wait_ge(s_x1m, b1 + 1)
                    after(pool, s_h2, b1)
                    g.tensor_tensor(tmp[:, 0, :], mom1[:, :, 0], neg_one[:, :], ALU.mult)
                    then(g.tensor_tensor(tmp[:, 1, :], mom1[:, :, 1], eps[:, :], ALU.add))
                    then(g.tensor_tensor(scale1[:, :], tmp[:, 1, :], neg_half[:, 0:TPB], ALU.pow))
                    g.tensor_tensor(shift1[:, :], tmp[:, 0, :], scale1[:, :], ALU.mult).then_inc(s_sc1, 1)
                if live(b2):
                    if isinstance(b2, int) and b2 == 0:
                        pool.wait_ge(s_tab, 1)
                    pool.wait_ge(s_u, b2 + 1)
                    after(pool, s_conv, b2)
                    g.tensor_tensor(vi, u, in_im, ALU.mult).then_inc(s_ui, 1)
                    if late:
                        scales()
                    pool.wait_ge(s_vi, b2 + 1)
                    g.tensor_tensor(vi, vi, out_im, ALU.mult).then_inc(s_ti, 1)
                if live(b1):
                    r = batch_of(resid, b1)
                    pool.wait_ge(s_x1, b1 + 1)
                    take_wait()
                    g.tensor_tensor(r, r, x1, ALU.add).then_inc(s_base, 1)
                if live(b3):
                    pool.wait_ge(s_sc0, b3 + 1)
                    after(pool, s_xn, b3)
                    then(g.tensor_tensor(tmp[:, 3, :], var_eps[:, 1, :], norm_pow[:, 1, :], ALU.mult))
                    g.tensor_tensor(unscale0[:, :, 0], tmp[:, 3, :], norm_pow[:, 0, :], ALU.mult).then_inc(s_un, 1)
                return ticks

            decay()
            base = iteration(-3, 0)
            pool.wait_ge(s_low_high, 1)
            g.tensor_tensor(grid(out_im), slow[0], fast[1], ALU.mult)
            g.tensor_tensor(grid(in_im), slow[1], fast[0], ALU.mult).then_inc(s_oim, 1)
            for i in range(-2, 1):
                base += iteration(i, base)
            whole = 2 + 2 + 1
            with pool.Fori(1, LAST - 3) as i:
                n = iteration(i, (i - 1) * whole + base)
                assert n == whole
            base += whole * (LAST - 4)
            for i in range(LAST - 3, LAST):
                base += iteration(i, base)

            def x2_scales(b, at):
                pool.wait_ge(s_x2m, b + 1)
                g.tensor_tensor(tmp[:, 6, :], mom2[:, :, 0], neg_one[:, :], ALU.mult)
                g.tensor_tensor(tmp[:, 7, :], mom2[:, :, 1], eps[:, :], ALU.add).then_inc(s_po, 1)
                pool.wait_ge(s_po, at + 1)
                g.tensor_tensor(scale2[:, :], tmp[:, 7, :], neg_half[:, 0:TPB], ALU.pow).then_inc(s_po, 1)
                pool.wait_ge(s_po, at + 2)
                g.tensor_tensor(shift2[:, :], tmp[:, 6, :], scale2[:, :], ALU.mult).then_inc(s_sc2, 1)

            def experts(n, q, more):
                for e in range(1, EXPERTS - 1 if isinstance(n, int) and n == LAST else EXPERTS):
                    pool.wait_ge(s_mul, n * (2 * EXPERTS) + (2 * e + 2))
                    after(pool, s_add, n * (EXPERTS - 1) + (e - 1))
                    g.tensor_tensor(total[q], total[q], part[e % 2], ALU.add).then_inc(s_add, 1)
                    if e == 3 and more:
                        x2_scales(n + 2, n * 2 + (base + 4))
            x2_scales(0, base)
            x2_scales(1, base + 2)
            experts(0, 0, True)
            with pool.Fori(0, (LAST - 3) // 2) as m:
                experts(m * 2 + 1, 1, True)
                experts(m * 2 + 2, 0, True)
            experts(LAST - 2, 1, True)
            experts(LAST - 1, 0, False)
            experts(LAST, 1, False)

        @block.scalar
        def _(a):
            s = nc.scalar
            a.wait_ge(s_par, 16)

            def load_table(function, k):
                s.activation(spare_a[:, k:k + 1], par[:, BETA:BETA + 1], function)
            load_table(ACT.Silu, 0)

            def iteration(i, to_e=False):
                b1, b2, b3 = i + 1, i + 2, i + 3

                def mlp_act(c):
                    a.wait_ge(s_up, i * FC + (c + 1))
                    after(a, s_dn, i * FC + (c - 1))
                    s.activation(silu[c % 2], up_p[c % 2][:, :], ACT.Silu, bias=b1_all[:, c:c + 1]).then_inc(s_silu, 1)
                if live(i):
                    mlp_act(0)
                    mlp_act(1)
                if live(b2):
                    a.wait_ge(s_t1, b2 + 1)
                    after(a, s_t2, b2)
                    s.activation(u, turn_p[:, :], ACT.Identity, bias=par[:, BETA:BETA + 1],
                                 scale=par[:, GAMMA:GAMMA + 1]).then_inc(s_u, 1)
                if live(b1):
                    a.wait_ge(s_sc1, b1 + 1)
                    after(a, s_t3, b1)
                    for j in range(TPB):
                        last = s.activation(h2[:, j, :], x1[:, j, :], ACT.Identity, bias=shift1[:, j:j + 1],
                                            scale=scale1[:, j:j + 1])
                    last.then_inc(s_h2, 1)
                if to_e:
                    high(0, 0)
                if live(i):
                    mlp_act(2)
                if to_e:
                    logits_copy(0)
                if live(b1):
                    a.wait_ge(s_t3, b1 + 1)
                    if live(i):
                        a.wait_ge(s_up, i * FC + FC)
                    s.activation(h_hi[:, :], turn_p[:, :], ACT.Copy).then_inc(s_hi, 1)
                if live(i):
                    mlp_act(3)
                if live(b3):
                    a.wait_ge(s_sc0, b3 + 1)
                    after(a, s_t1, b3)
                    after(a, s_xn, b3)
                    for j in range(TPB):
                        last = s.activation(hn[:, j, :], tile_of(resid, b3, j), ACT.Identity, bias=shift0[:, j:j + 1],
                                            scale=norm_pow[:, 1, j:j + 1])
                    last.then_inc(s_hn, 1)
                if to_e:
                    load_table(ACT.Gelu, 1)
                    norm(1)
                    tanh(0)

            def norm(b, part=None):
                if part in (None, 0):
                    a.wait_ge(s_sc2, b + 1)
                    after(a, s_t4, b)
                tiles = range(TPB) if part is None else range(part * TPB // 4, (part + 1) * TPB // 4)
                for j in tiles:
                    last = s.activation(xm[:, j, :], tile_of(resid, b, j), ACT.Identity, bias=shift2[:, j:j + 1],
                                        scale=scale2[:, j:j + 1])
                if part in (None, 3):
                    last.then_inc(s_xm, 1)

            def high(b, q):
                a.wait_ge(s_t4, b + 1)
                after(a, s_mup, b * (EC * EXPERTS) - EC * EXPERTS)
                s.activation(xm_hi[q][:, :], turn_p[:, :], ACT.Copy).then_inc(s_xhi, 1)

            def logits_copy(b):
                a.wait_ge(s_rt, b + 1)
                s.activation(logit_t, turn_p[0:EXPERTS, :], ACT.Copy).then_inc(s_lt, 1)

            def tanh(b):
                a.wait_ge(s_gap, b + 1)
                s.activation(th[:, :, :], gap[:, :, :], ACT.Tanh, scale=0.5).then_inc(s_tanh, 1)

            def comb_copy(b):
                a.wait_ge(s_cm, b + 1)
                after(a, s_cd, b * 16)
                s.activation(comb_t, turn_p[0:EXPERTS, :], ACT.Copy).then_inc(s_ct, 1)

            def expert_weights():
                a.wait_ge(s_mw, 16 * 2)
                s.activation(mw2_hi[:, :], mw2_sb, ACT.Copy)
                s.activation(mw1_hi[:, :], mw1_sb, ACT.Copy).then_inc(s_mwhi, 1)

            a.wait_ge(s_w, 16 * 4)
            a.wait_ge(s_ident, 1)
            s.activation(b2_hi, b2_rows, ACT.Copy).then_inc(s_aw, 1)
            s.activation(w1_g, w1_sb, ACT.Copy, scale=par[:, GAMMA:GAMMA + 1]).then_inc(s_aw, 1)
            a.wait_ge(s_aw, 1)
            s.activation(b2_first, b2_hi.bitcast(f32), ACT.Copy, scale=ident[0:2, 0:1])
            a.wait_ge(s_aw, 2)
            s.activation(w1_hi[:, :], w1_g, ACT.Copy).then_inc(s_whi, 1)
            iteration(-3)
            a.wait_ge(s_ore, 1)
            s.activation(in_re, out_re, ACT.Copy, scale=par[:, INIT_RE:INIT_RE + 1])
            s.activation(vi, out_re, ACT.Copy, scale=par[:, INIT_IM:INIT_IM + 1]).then_inc(s_ire, 1)
            for i in range(-2, 0):
                iteration(i)
            a.wait_ge(s_b1, 1)
            iteration(0)
            with a.Fori(1, LAST - 3) as i:
                iteration(i)
            for i in range(LAST - 3, LAST - 2):
                iteration(i)
            iteration(LAST - 2)
            expert_weights()
            iteration(LAST - 1)
            norm(0)
            iteration(LAST, True)

            def gelu(n, e, c):
                a.wait_ge(s_mup, n * (EC * EXPERTS) + (EC * e + c + 1))
                after(a, s_elo, n * (EC * EXPERTS) + (EC * (e - 2) + c + 1))
                k = MB1 + e * EC + c
                s.activation(hid[c][e % 2], up_p[c][:, :], ACT.Gelu, bias=par[:, k:k + 1]).then_inc(s_gelu, 1)

            def hid_high(n, e, c, done):
                a.wait_ge(s_gelu, n * (EC * EXPERTS) + (EC * e + c + 1))
                after(a, s_edn, n * (2 * EXPERTS) + 2 * (e - 1))
                s.activation(hid_hi[c][e % 2][:, :], hid[c][e % 2], ACT.Copy).then_inc(done, 1)

            def both(n, e, first=None, second=None):
                gelu(n, e, 0)
                hid_high(n, e, 0, s_hi0)
                if first is not None:
                    first()
                gelu(n, e, 1)
                if second is not None:
                    second()
                hid_high(n, e, 1, s_hi1)

            def experts(n, q, more, second):
                for e in range(EXPERTS):
                    if more:
                        if e == Step.split:
                            high(n + 1, 1 - q)
                        if e == Step.logits:
                            logits_copy(n + 1)
                    between = (lambda: tanh(n + 1)) if more and e == Step.probabilities else None
                    after_second = (lambda: comb_copy(n + 1)) if more and e == Step.weights else None
                    if e + 1 < EXPERTS:
                        both(n, e + 1, between, after_second)
                    elif more:
                        both(n + 1, 0, between, after_second)
                    if second and e >= 4:
                        norm(n + 2, e - 4)
            both(0, 0, None, lambda: comb_copy(0))
            experts(0, 0, True, True)
            with a.Fori(0, (LAST - 3) // 2) as m:
                experts(m * 2 + 1, 1, True, True)
                experts(m * 2 + 2, 0, True, True)
            experts(LAST - 2, 1, True, True)
            experts(LAST - 1, 0, True, False)
            experts(LAST, 1, False, False)

        @block.tensor
        def _(pe):
            t = nc.tensor

            def turned(src, done):
                for j in range(TPB):
                    last = t.transpose(turn_p[:, j * TILE:(j + 1) * TILE], src(j), ident[:, :])
                last.then_inc(done, 1)

            def split_product(dst, terms, done=None):
                for k, (w_hi, w_lo, x_hi, x_lo) in enumerate(terms):
                    t.matmul(dst, w_hi, x_lo, start=k == 0, stop=False)
                    t.matmul(dst, w_hi, x_hi, start=False, stop=False)
                    last = t.matmul(dst, w_lo, x_hi, start=False, stop=k == len(terms) - 1)
                if done is not None:
                    last.then_inc(done, 1)

            def up(dst, hi, lo, w_hi, w_lo, done):
                for h in range(2):
                    split_product(half(dst, h), [(w_hi, w_lo, half(hi, h), half(lo, h))], done if h else None)

            def mlp_up(i, c):
                after(pe, s_silu, i * FC + (c - 1))
                k = slice(c * 128, (c + 1) * 128)
                up(up_p[c % 2], h_hi, h_lo, w1_hi[:, k], w1_lo[:, k], s_up)

            def mlp_down(i, c):
                if c == 0:
                    after(pe, s_x2, i)
                    for h in range(2):
                        t.matmul(half(down_p, h), ones[:, :], b2_hi_lo[:, :], start=True, stop=False,
                                 skip_group_check=True)
                pe.wait_ge(s_silu, i * FC + (c + 1))
                for j in range(TPB):
                    last = t.matmul(down_p[:, j * D:(j + 1) * D], silu[c % 2][:, j * TILE:(j + 1) * TILE],
                                    w2_sb[:, c, :], start=False, stop=c == FC - 1, skip_group_check=True)
                last.then_inc(s_dn, 1)

            def iteration(i, to_e=False):
                b1, b2 = i + 1, i + 2
                early = isinstance(i, int) and i == 0
                if early:
                    pe.wait_ge(s_lo, i + 1)
                    mlp_up(i, 0)
                if live(b1):
                    pe.wait_ge(s_conv, b1 + 1)
                    after(pe, s_lo, b1)
                    turned(lambda j: u[:, j * TILE:(j + 1) * TILE], s_t2)
                if live(i):
                    if not early:
                        pe.wait_ge(s_lo, i + 1)
                        mlp_up(i, 0)
                    mlp_up(i, 1)
                if live(b2):
                    pe.wait_ge(s_hn, b2 + 1)
                    after(pe, s_x1, b2)
                    turned(lambda j: hn[:, j, :], s_t1)
                if to_e:
                    xm_turn(0)
                if live(i):
                    mlp_down(i, 0)
                    mlp_up(i, 2)
                    if to_e:
                        route(0, 0)
                    mlp_down(i, 1)
                    mlp_up(i, 3)
                    if to_e:
                        logits_turn(0)
                if live(b1):
                    pe.wait_ge(s_h2, b1 + 1)
                    if live(b2):
                        pe.wait_ge(s_u, b2 + 1)
                    turned(lambda j: h2[:, j, :], s_t3)
                if live(i):
                    mlp_down(i, 2)
                    if to_e:
                        expert_up(0, 0, 0)
                    mlp_down(i, 3)

            def xm_turn(b):
                pe.wait_ge(s_xm, b + 1)
                after(pe, s_ct, b)
                if isinstance(b, int) and b == 0:
                    pe.wait_ge(s_lo, BATCHES)
                turned(lambda j: xm[:, j, :], s_t4)

            def route(b, q):
                pe.wait_ge(s_xlo, b + 1)
                up(turn_p, xm_hi[q], xm_lo[q], router_hi[:, :], router_lo[:, :], s_rt)

            def logits_turn(b):
                pe.wait_ge(s_lt, b + 1)
                for j in range(TPB):
                    dst, src = turn_p[:, j * EXPERTS:(j + 1) * EXPERTS], logit_t[:, j * TILE:(j + 1) * TILE]
                    if j == 0:
                        last = t.matmul(dst, src, ident[0:EXPERTS, 0:EXPERTS], start=True, stop=True)
                    else:
                        last = t.transpose(dst, src, ident[0:EXPERTS, 0:EXPERTS])
                last.then_inc(s_tn, 1)

            def comb_turn(b):
                pe.wait_ge(s_comb, b + 1)
                after(pe, s_out, b - 1)
                for j in range(TPB):
                    last = t.transpose(turn_p[0:EXPERTS, j * TILE:(j + 1) * TILE], comb[:, j, :], ident[:, :])
                last.then_inc(s_cm, 1)

            def total_turn(n, q, routing):
                pe.wait_ge(s_add, n * (EXPERTS - 1) + (EXPERTS - 1))
                if routing:
                    pe.wait_ge(s_lg, n + 3)
                else:
                    pe.wait_ge(s_ct, n + 2)
                turned(lambda j: total[q][:, j * TILE:(j + 1) * TILE], s_otr)

            def expert_up(n, e, q):
                if e == 0:
                    pe.wait_ge(s_xlo, n + 1)
                for c in range(EC):
                    if isinstance(n, int) and n == 0 and e == 0:
                        pe.wait_ge(s_silu, BATCHES * FC - EC + c + 1)
                    after(pe, s_gelu, n * (EC * EXPERTS) + (EC * (e - 1) + c + 1))
                    k = slice((e * EC + c) * 128, (e * EC + c + 1) * 128)
                    up(up_p[c], xm_hi[q], xm_lo[q], mw1_hi[:, k], mw1_lo[:, k], s_mup)

            pe.wait_ge(s_ident, 1)
            pe.wait_ge(s_w, 16 * 4)
            pe.wait_ge(s_par, 16)
            for c in range(FC):
                last = t.matmul(down_p[:, c:c + 1], w1_sb[:, c * 128:(c + 1) * 128], par[:, BETA:BETA + 1],
                                start=True, stop=True)
            last.then_inc(s_b1raw, 1)
            for i in range(-2, 0):
                iteration(i)
            pe.wait_ge(s_wsplit, 1)
            pe.wait_ge(s_b1, 1)
            iteration(0)
            with pe.Fori(1, LAST - 3) as i:
                iteration(i)
            for i in range(LAST - 3, LAST):
                iteration(i)
            iteration(LAST, True)

            def expert_down(n, e):
                if isinstance(n, int) and n == 0 and e == 0:
                    pe.wait_ge(s_x2, BATCHES)
                pe.wait_ge(s_elo, n * (EC * EXPERTS) + (EC * e + EC))
                for h in range(2):
                    after(pe, s_mul, n * (2 * EXPERTS) + (2 * (e - 1) + h + 1))
                    terms = []
                    for c in range(EC):
                        k = slice((e * EC + c) * D, (e * EC + c + 1) * D)
                        terms.append((mw2_hi[:, k], mw2_lo[:, k], half(hid_hi[c][e % 2], h), half(hid_lo[c][e % 2], h)))
                    split_product(half(down_p, h), terms, s_edn)

            def experts(n, q, before, more):
                for e in range(EXPERTS):
                    if e + 1 < EXPERTS:
                        expert_up(n, e + 1, q)
                    elif more:
                        expert_up(n + 1, 0, 1 - q)
                    if more:
                        if e == Step.turn:
                            xm_turn(n + 1)
                        if e == Step.weights:
                            comb_turn(n + 1)
                    if e == Step.total and before:
                        total_turn(n - 1, 1 - q, more)
                    expert_down(n, e)
                    if more:
                        if e == Step.split:
                            route(n + 1, 1 - q)
                        if e == Step.logits:
                            logits_turn(n + 1)
            comb_turn(0)
            experts(0, 0, False, True)
            with pe.Fori(0, (LAST - 3) // 2) as m:
                experts(m * 2 + 1, 1, True, True)
                experts(m * 2 + 2, 0, True, True)
            experts(LAST - 2, 1, True, True)
            experts(LAST - 1, 0, True, True)
            experts(LAST, 1, True, False)
            pe.wait_ge(s_out, LAST)
            for h in range(2):
                pe.wait_ge(s_last, h + 1)
                for j in range(TPB)[some(h)]:
                    last = t.transpose(turn_p[:, j * TILE:(j + 1) * TILE], total[1][:, j * TILE:(j + 1) * TILE],
                                       ident[:, :])
                last.then_inc(s_lotr, 1)

        @block.vector
        def _(v):
            d = nc.vector
            made, taken = [0], [0]

            def link(ins, meanwhile=None):
                made[0] += 1
                ins.then_inc(s_vc, 1)
                if meanwhile is not None:
                    meanwhile()
                v.wait_ge(s_vc, made[0])

            def take_wait():
                taken[0] += 1
                k = taken[0] % SPARE
                d.memset(spare_v[:, k:k + 1], 0.0)

            def statistics(src, stats, tiles=range(TPB)):
                take_wait()
                for j in tiles:
                    last = d.bn_stats(stats[:, j, :], src(j))
                return last

            def aggregates(stats, mom, done):
                take_wait()
                for j in range(TPB):
                    last = d.bn_aggr(mom[:, j, :], stats[:, j, :])
                last.then_inc(done, 1)

            def moments(src, stats, mom, at, done):
                statistics(src, stats).then_inc(s_vo, 1)
                v.wait_ge(s_vo, at + 1)
                aggregates(stats, mom, done)

            def iteration(i, base, to_e=False):
                ticks = 0
                first, second = (isinstance(i, int) and i == k for k in (-2, -1))
                b0, b1, b2, b3, b4 = i - 1, i + 1, i + 2, i + 3, i + 4

                def then(ins):
                    nonlocal ticks
                    ins.then_inc(s_vo, 1)
                    ticks += 1
                    v.wait_ge(s_vo, base + ticks)
                if live(b0):
                    v.wait_ge(s_dn, i * FC)
                    v.wait_ge(s_base, i)
                    r = batch_of(resid, b0)
                    d.tensor_tensor(r, tiled(down_p[:, :]), r, ALU.add).then_inc(s_x2, 1)
                if live(b1):
                    v.wait_ge(s_t2, b1 + 1)
                    v.wait_ge(s_xn, b1 + 1)
                    after(v, s_base, b1)
                    after(v, s_h2, b1)
                    d.tensor_tensor(x1, xn, tiled(turn_p[:, :]), ALU.add).then_inc(s_x1, 1)
                    v.wait_ge(s_x1, b1 + 1)
                    after(v, s_sc1, b1)
                    moments(lambda j: x1[:, j, :], stats1, mom1, base + ticks, s_x1m)
                    ticks += 1

                def x_statistics(b):
                    nonlocal ticks
                    v.wait_ge(s_x, b * 16 + 16)
                    after(v, s_x0m, b)
                    statistics(lambda j: tile_of(resid, b, j), stats0).then_inc(s_vo, 1)
                    ticks += 1

                def x_moments(b, at):
                    v.wait_ge(s_vo, at)
                    after(v, s_sc0, b)
                    aggregates(stats0, mom0, s_x0m)

                def rotate(between=None):
                    nonlocal ticks
                    decay = decay_factor.to_broadcast([128, LENGTH])
                    v.wait_ge(s_u, b2 + 1)
                    d.tensor_tensor(vr, u, in_re, ALU.mult).then_inc(s_vo, 1)
                    ticks += 1
                    rotated = base + ticks
                    if between is not None:
                        between()
                    v.wait_ge(s_vo, rotated)
                    then(d.tensor_tensor_scan(vr, decay, vr, start_v[:, 0:1], ALU.mult, ALU.add))
                    v.wait_ge(s_ui, b2 + 1)
                    d.tensor_tensor_scan(vi, decay, vi, start_v[:, 1:2], ALU.mult, ALU.add).then_inc(s_vi, 1)
                    then(d.tensor_tensor(vr, vr, out_re, ALU.mult))

                def convolution():
                    v.wait_ge(s_ti, b2 + 1)
                    d.tensor_tensor(u, vr, vi, ALU.subtract).then_inc(s_conv, 1)
                if first:
                    rotate()
                m = b3 if second else b4
                moments_here = live(b4) and not first
                if moments_here:
                    x_statistics(m)
                    counted = base + ticks
                if live(b2):
                    v.wait_ge(s_hn, b2 + 1)
                    v.wait_ge(s_un, b2 + 1)
                    d.tensor_tensor(xn, hn, unscale0[:, :, :].to_broadcast([128, TPB, D]), ALU.mult).then_inc(s_xn, 1)
                if first:
                    convolution()
                if to_e:
                    x2_stats(0, None, base + ticks)
                    expert_weights()
                if live(b2) and not first:
                    rotate((lambda: x_moments(m, counted)) if moments_here else None)
                elif moments_here:
                    x_moments(m, counted)
                if live(b1):
                    v.wait_ge(s_hi, b1 + 1)
                    d.tensor_tensor(h_lo[:, :], turn_p[:, :], h_hi[:, :].bitcast(f32), ALU.subtract).then_inc(s_lo, 1)
                if live(b2) and not first:
                    convolution()
                if second:
                    x_statistics(b4)
                    x_moments(b4, base + ticks)
                return ticks

            def weights():
                v.wait_ge(s_whi, 1)
                link(d.tensor_tensor(b2_lo, b2_rows, b2_hi.bitcast(f32), ALU.subtract))
                d.scalar_tensor_tensor(out=b2_hi_lo[:, :], in0=b2_lo, scalar=ident[0:2, 1:2], in1=b2_first,
                                       op0=ALU.mult, op1=ALU.add)
                d.tensor_tensor(w1_lo[:, :], w1_g, w1_hi[:, :].bitcast(f32), ALU.subtract).then_inc(s_wsplit, 1)
                v.wait_ge(s_b1raw, 1)
                d.tensor_tensor(b1_all[:, :], down_p[:, 0:FC], par[:, B1:B1 + FC], ALU.add).then_inc(s_b1, 1)

            def expert_weights():
                v.wait_ge(s_mw, 16 * 2)
                d.memset(router_hi[:, :].bitcast(f32), 0.0)
                link(d.memset(router_lo[:, :].bitcast(f32), 0.0))
                link(d.tensor_copy(router_hi[:, 0:EXPERTS], router_sb[:, :]))
                v.wait_ge(s_mwhi, 1)
                d.tensor_tensor(router_lo[:, 0:EXPERTS], router_sb[:, :], router_hi[:, 0:EXPERTS].bitcast(f32),
                                ALU.subtract)
                d.tensor_tensor(mw2_lo[:, :], mw2_sb, mw2_hi[:, :].bitcast(f32), ALU.subtract)
                d.tensor_tensor(mw1_lo[:, :], mw1_sb, mw1_hi[:, :].bitcast(f32), ALU.subtract).then_inc(s_wsplit, 1)
                for e in range(EXPERTS):
                    last = d.memset(rank[:, :, e:e + 1], float(EXPERTS - e))
                link(last)

            def tables(early, between):
                v.wait_ge(s_mag, 1)
                link(d.reciprocal(inv_abs[:, :], abs_p))
                link(d.tensor_scalar(zz[:, 0, :], par[:, P_RE:P_RE + 2], inv_abs[:, :], None, ALU.mult))
                for k in range(1, POWERS):
                    d.tensor_tensor(sq[:, 0:2], zz[:, k - 1, :], zz[:, k - 1, :], ALU.mult)
                    last = d.tensor_tensor(sq[:, 2:3], zz[:, k - 1, 0:1], zz[:, k - 1, 1:2], ALU.mult)
                    link(last, lambda: early(k))
                    d.tensor_tensor(zz[:, k, 0:1], sq[:, 0:1], sq[:, 1:2], ALU.subtract)
                    link(d.tensor_scalar(zz[:, k, 1:2], sq[:, 2:3], 2.0, None, ALU.mult))
                    if k % 2 == 0 or k == POWERS - 1:
                        link(d.tensor_tensor(sq[:, 0:2], zz[:, k, :], zz[:, k, :], ALU.mult))
                        link(d.tensor_tensor(sq[:, 3:4], sq[:, 0:1], sq[:, 1:2], ALU.add))
                        link(d.tensor_scalar(sq[:, 3:4], sq[:, 3:4], -0.5, 1.5, ALU.mult, ALU.add))
                        link(d.tensor_scalar(zz[:, k, :], zz[:, k, :], sq[:, 3:4], None, ALU.mult))
                link(d.tensor_scalar(start_v[:, 0:2], par[:, LAST_RE:LAST_RE + 2], zz[:, 0, 0:1], None, ALU.mult))
                link(d.tensor_scalar(start_v[:, 2:4], par[:, LAST_RE:LAST_RE + 2], zz[:, 0, 1:2], None, ALU.mult))
                d.tensor_tensor(start_v[:, 0:1], start_v[:, 0:1], start_v[:, 3:4], ALU.subtract)
                d.tensor_tensor(start_v[:, 1:2], start_v[:, 1:2], start_v[:, 2:3], ALU.add)
                re, im = low_high[:, 0, :, :], low_high[:, 1, :, :]
                d.memset(re[:, :, 0:1], 1.0)
                link(d.memset(im[:, :, 0:1], 0.0))
                d.tensor_scalar(neg_init_re[:, :], par[:, INIT_RE:INIT_RE + 1], -1.0, None, ALU.mult)
                n, k = 1, 0
                while n < STEP:
                    z_re = zz[:, k::POWERS // 2, 0:1].to_broadcast([128, 2, n])
                    z_im = zz[:, k::POWERS // 2, 1:2].to_broadcast([128, 2, n])
                    p = [prod[:, m, :, 0:n] for m in range(4)]
                    d.tensor_tensor(p[0], re[:, :, 0:n], z_re, ALU.mult)
                    d.tensor_tensor(p[1], im[:, :, 0:n], z_im, ALU.mult)
                    d.tensor_tensor(p[2], re[:, :, 0:n], z_im, ALU.mult)
                    link(d.tensor_tensor(p[3], im[:, :, 0:n], z_re, ALU.mult))
                    d.tensor_tensor(re[:, :, n:2 * n], p[0], p[1], ALU.subtract)
                    last = d.tensor_tensor(im[:, :, n:2 * n], p[2], p[3], ALU.add)
                    n, k = 2 * n, k + 1
                    if n < STEP:
                        link(last)
                last.then_inc(s_low_high, 1)
                v.wait_ge(s_low_high, 1)
                d.tensor_tensor(grid(out_re), slow[0], fast[0], ALU.mult)
                link(d.tensor_tensor(grid(vr), slow[1], fast[1], ALU.mult))
                d.tensor_tensor(out_re, out_re, vr, ALU.subtract).then_inc(s_ore, 1)
                between()
                v.wait_ge(s_oim, 1)
                link(d.tensor_tensor(out_im, out_im, in_im, ALU.add))
                v.wait_ge(s_ire, 1)
                d.scalar_tensor_tensor(out=in_im, in0=out_im, scalar=neg_init_re[:, :], in1=vi,
                                       op0=ALU.mult, op1=ALU.add)
                d.scalar_tensor_tensor(out=in_re, in0=out_im, scalar=par[:, INIT_IM:INIT_IM + 1], in1=in_re,
                                       op0=ALU.mult, op1=ALU.add).then_inc(s_tab, 1)

            SOME = 5

            def x2_stats(b, part=None, at=None):
                src = lambda j: tile_of(resid, b, j)
                if part != 1:
                    v.wait_ge(s_x2, b + 1)
                    after(v, s_sc2, b)
                    last = statistics(src, stats2, range(TPB if part is None else SOME))
                if part == 1:
                    last = statistics(src, stats2, range(SOME, TPB))
                if part != 0:
                    last.then_inc(s_vo, 1)
                    v.wait_ge(s_vo, b + ((base if at is None else at) + 1))
                    aggregates(stats2, mom2, s_x2m)

            def first_moments(k):
                if k == 2:
                    v.wait_ge(s_x, 16)
                    take_wait()
                if 2 <= k < 2 + TPB // 2:
                    for j in range(2 * (k - 2), 2 * (k - 1)):
                        last = d.bn_stats(stats0[:, j, :], resid[:, j, :])
                    if k == 1 + TPB // 2:
                        last.then_inc(s_vo, 1)
                if k == 2 + TPB // 2:
                    v.wait_ge(s_vo, 1)
                    aggregates(stats0, mom0, s_x0m)
            v.wait_ge(s_par, 16)
            base = 1
            tables(first_moments, lambda: iteration(-3, base))
            base += 1
            v.wait_ge(s_decay, 1)
            v.wait_ge(s_tab, 1)
            base += iteration(-2, base)
            weights()
            base += iteration(-1, base)
            base += iteration(0, base)
            whole = 1 + 1 + 3
            with v.Fori(1, LAST - 3) as i:
                n = iteration(i, (i - 1) * whole + base)
                assert n == whole, n
            base += whole * (LAST - 4)
            for i in range(LAST - 3, LAST - 1):
                base += iteration(i, base)
            base += iteration(LAST - 1, base, True)

            def low(b, q):
                v.wait_ge(s_xhi, b + 1)
                d.tensor_tensor(xm_lo[q][:, :], turn_p[:, :], xm_hi[q][:, :].bitcast(f32), ALU.subtract)\
                    .then_inc(s_xlo, 1)

            def wide(ap):
                return ap.to_broadcast([128, TPB, EXPERTS])
            ORDER = 5 + 1 + 5 + 3

            class Choice:
                def __init__(self, b):
                    self.b, self.ticks = b, 0

                def then(self, ins):
                    ins.then_inc(s_tv, 1)
                    self.ticks += 1
                    v.wait_ge(s_tv, self.b * ORDER + self.ticks)

                def choose(self, top, onehot):
                    then = self.then
                    then(d.tensor_reduce(top[:, :, :], logits[:, :, :], AX, ALU.max))
                    then(d.tensor_tensor(scored[:, :, :], logits[:, :, :], wide(top[:, :, :]), ALU.is_equal))
                    then(d.tensor_tensor(scored[:, :, :], scored[:, :, :], wide(rank[:, :, :]), ALU.mult))
                    then(d.tensor_reduce(pick[:, :, :], scored[:, :, :], AX, ALU.max))
                    then(d.tensor_tensor(onehot[:, :, :], scored[:, :, :], wide(pick[:, :, :]), ALU.is_equal))

                def choose_first(self):
                    v.wait_ge(s_tn, self.b + 1)
                    d.tensor_copy(logits[:, :, :], turn_p[:, 0:TPB * EXPERTS].rearrange("p (t e) -> p t e", e=EXPERTS))\
                        .then_inc(s_lg, 1)
                    v.wait_ge(s_lg, self.b + 1)
                    self.choose(best, first)
                    self.then(d.scalar_tensor_tensor(out=logits[:, :, :], in0=first[:, :, :], scalar=-LARGE,
                                                     in1=logits[:, :, :], op0=ALU.mult, op1=ALU.add))

                def choose_second(self):
                    self.choose(runner, second)
                    d.tensor_tensor(gap[:, :, :], best[:, :, :], runner[:, :, :], ALU.subtract).then_inc(s_gap, 1)

                def probabilities(self):
                    v.wait_ge(s_tanh, self.b + 1)
                    after(v, s_cm, self.b)
                    d.tensor_scalar(prob[:, 0, :, :], th[:, :, :], 0.5, 0.5, ALU.mult, ALU.add)
                    self.then(d.tensor_scalar(prob[:, 1, :, :], th[:, :, :], -0.5, 0.5, ALU.mult, ALU.add))
                    self.then(d.tensor_tensor(first[:, :, :], first[:, :, :], wide(prob[:, 0, :, :]), ALU.mult))
                    self.then(d.tensor_tensor(second[:, :, :], second[:, :, :], wide(prob[:, 1, :, :]), ALU.mult))
                    d.tensor_tensor(comb[:, :, :], first[:, :, :], second[:, :, :], ALU.add).then_inc(s_comb, 1)
                    assert self.ticks == ORDER, self.ticks

            iteration(LAST, base)
            low(0, 0)
            x2_stats(1)
            c = Choice(0)
            c.choose_first()
            c.choose_second()
            c.probabilities()

            def hid_low(n, e, c):
                v.wait_ge((s_hi0, s_hi1)[c], n * EXPERTS + (e + 1))
                d.tensor_tensor(hid_lo[c][e % 2][:, :], hid[c][e % 2], hid_hi[c][e % 2][:, :].bitcast(f32),
                                ALU.subtract).then_inc(s_elo, 1)

            def scaled(n, q, e, h):
                if h == 0:
                    v.wait_ge(s_cb[e], n * 16 + 16)
                    if e > 0:
                        after(v, s_add, n * (EXPERTS - 1) + max(e - 2, 0))
                v.wait_ge(s_edn, n * (2 * EXPERTS) + (2 * e + h + 1))
                d.scalar_tensor_tensor(out=half(part[e % 2] if e else total[q], h), in0=half(down_p, h),
                                       scalar=par[:, MB2 + e:MB2 + e + 1], in1=half(weight[e], h),
                                       op0=ALU.add, op1=ALU.mult).then_inc(s_mul, 1)

            def finish(n):
                v.wait_ge(s_otr, n + 1)
                d.tensor_tensor(result, tiled(turn_p[:, :]), batch_of(resid, n), ALU.add).then_inc(s_out, 1)

            def experts(n, q, before, more, second):
                if more:
                    c = Choice(n + 1)
                for e in range(EXPERTS):
                    if more and e == Step.split:
                        low(n + 1, 1 - q)
                    if before and e == Step.finish:
                        finish(n - 1)
                    for h in range(2):
                        if e + 1 < EXPERTS:
                            hid_low(n, e + 1, h)
                        elif more:
                            hid_low(n + 1, 0, h)
                        scaled(n, q, e, h)
                        if more and e == Step.probabilities and h == 0:
                            c.probabilities()
                        if not more and e == EXPERTS - 1:
                            if h == 0:
                                v.wait_ge(s_add, BATCHES * (EXPERTS - 1) - 1)
                            v.wait_ge(s_mul, BATCHES * 2 * EXPERTS - 1 + h)
                            d.tensor_tensor(half(total[q], h), half(total[q], h), half(part[e % 2], h), ALU.add)\
                                .then_inc(s_last, 1)
                    if more:
                        if e == Step.first:
                            c.choose_first()
                        if e == Step.second:
                            c.choose_second()
                    if second and e in (0, 2):
                        x2_stats(n + 2, e // 2)
            hid_low(0, 0, 0)
            iteration(LAST + 1, base)
            hid_low(0, 0, 1)
            experts(0, 0, False, True, True)
            with v.Fori(0, (LAST - 3) // 2) as m:
                experts(m * 2 + 1, 1, True, True, True)
                experts(m * 2 + 2, 0, True, True, True)
            experts(LAST - 2, 1, True, True, True)
            experts(LAST - 1, 0, True, True, False)
            experts(LAST, 1, True, False, False)
            v.wait_ge(s_store, LAST * 16)
            for h in range(2):
                v.wait_ge(s_lotr, h + 1)
                d.tensor_tensor(result[:, some(h), :], tiled(turn_p[:, :])[:, some(h), :],
                                batch_of(resid, LAST)[:, some(h), :], ALU.add).then_inc(s_out, 1)


def kernel(**inputs):
    import numpy as np
    import concourse.bacc as bacc
    from concourse.bass_utils import run_bass_kernel_spmd

    p = {k: np.asarray(v) for k, v in inputs.items()}
    a, f = "L0_attn_", "L0_ffn_"
    columns = [p[a + k][:, None] for k in ("ln_gamma", "ln_beta", "phazor_re", "phazor_im", "phazor_init_re",
                                           "phazor_init_im", "last_conv_re", "last_conv_im")]
    columns.append(p[a + "b1"].reshape(FC, 128).T)
    columns.append(p[f + "b1"].reshape(EXPERTS * EC, 128).T)
    columns.append(p[f + "b2"].T)
    arrays = {
        "x": p[a + "x"],
        "cols": np.concatenate(columns, axis=1),
        "w1": p[a + "w1"],
        "w2": p[a + "w2"],
        "b2": np.tile(p[a + "b2"], (2, HALF // D)),
        "router": p[f + "router_w"].T,
        "mw1": p[f + "w1"].reshape(EXPERTS * EF, D).T,
        "mw2": p[f + "w2"].transpose(0, 2, 1),
    }
    arrays = {f"in_{k}": np.ascontiguousarray(v) for k, v in arrays.items()}
    nc = bacc.Bacc("TRN2", target_bir_lowering=False, num_devices=1)
    args = [nc.dram_tensor(k, v.shape, mybir.dt.from_np(v.dtype), kind="ExternalInput").ap()
            for k, v in arrays.items()]
    args.append(nc.dram_tensor("out", (BATCHES, LENGTH, D), mybir.dt.float32, kind="ExternalOutput").ap())
    block_moe_kernel(nc, *args)
    return run_bass_kernel_spmd(nc, [arrays], core_ids=[0]).results[0]["out"]
```
